# Optimizing a Trainium2 kernel written in Bass

```python
import numpy as np
import jax
import jax.numpy as jnp

def _softmax(x, axis=-1):
    return jax.nn.softmax(x, axis=axis)

def _gelu(x):
    return jax.nn.gelu(x, approximate=True)

def _silu(x):
    return jax.nn.silu(x)

def _sigmoid(x):
    return jax.nn.sigmoid(x)

def _layernorm(x, axis=-1, eps=1e-05):
    m = jnp.mean(x, axis=axis, keepdims=True)
    v = jnp.var(x, axis=axis, keepdims=True)
    return (x - m) / jnp.sqrt(v + eps)

def _scatter_add(tgt, idx, src, axis=0):
    return tgt.at[idx].add(src)

def _segment_sum(src, seg, n):
    return jax.ops.segment_sum(src, seg, n)
kernel_name = 'mk_vit_tower_d1_tok_img768_r4_74b49c'

def setup_inputs(seed: int=0):
    np.random.seed(seed)
    _w = jnp.asarray

    def _rec_inputs():
        import jax
        import jax.numpy as jnp
        _rk = jax.random.key(seed)
        x = 7.57192e-06 + 1.00007 * jax.random.normal(jax.random.fold_in(_rk, 1), (64, 3, 224, 224), jnp.float32)
        return x
    x = _rec_inputs()

    def _L0_tok_setup():
        import jax, jax.numpy as jnp
        import numpy as np
        IMG = 224
        PATCH = 16
        C_IN = 3
        EMBED = 192
        PATCH_DIM = C_IN * PATCH * PATCH
        BATCH = 64

        def _layernorm(h, gamma, beta, eps=1e-05):
            mu = jnp.mean(h, axis=-1, keepdims=True)
            var = jnp.mean(jnp.square(h - mu), axis=-1, keepdims=True)
            return (h - mu) * jax.lax.rsqrt(var + eps) * gamma + beta
        key = jax.random.key(seed)
        k1, k2 = jax.random.split(key)
        x = jax.random.normal(k1, (BATCH, C_IN, IMG, IMG), dtype=jnp.float32)
        w_proj = jax.random.normal(k2, (PATCH_DIM, EMBED), dtype=jnp.float32) / np.sqrt(PATCH_DIM)
        b_proj = jnp.zeros((EMBED,), dtype=jnp.float32)
        ln_gamma = jnp.ones((EMBED,), dtype=jnp.float32)
        ln_beta = jnp.zeros((EMBED,), dtype=jnp.float32)
        return {'x': x, 'w_proj': w_proj, 'b_proj': b_proj, 'ln_gamma': ln_gamma, 'ln_beta': ln_beta}
    _L0_tok_all = _L0_tok_setup()
    _L0_tok_in = {k: v for k, v in _L0_tok_all.items() if k in ('w_proj', 'b_proj', 'ln_gamma', 'ln_beta')}
    del _L0_tok_all

    def _L0_attn_setup():
        import jax, jax.numpy as jnp
        import numpy as np
        NUM_HEADS = 12

        def _l2_norm(t):
            return t / jnp.linalg.norm(t, axis=-2, keepdims=True)

        def _reference_tuple_inner(x, w_qkv, w_proj, b_proj):
            B, N, C = x.shape
            H = NUM_HEADS
            D = C // H
            qkv = (x @ w_qkv).reshape(B, N, 3, H, D).transpose(2, 0, 3, 1, 4)
            q, k, v = (qkv[0], qkv[1], qkv[2])
            q = _l2_norm(q)
            kT = _l2_norm(k).transpose(0, 1, 3, 2)
            sum_k = kT.sum(axis=-1)
            D_inv = 1.0 / (N + jnp.einsum('bhnd,bhd->bhd', q, sum_k))
            attn_matrix = jnp.einsum('bhnd,bhdn->bhdn', q, kT) * D_inv[..., None]
            matrix = jnp.einsum('bhnd,bhdn->bdhn', v, kT)
            y = jnp.einsum('bdhn,bhdn->bhnd', matrix, attn_matrix)
            y = y.transpose(0, 2, 1, 3).reshape(B, N, C)
            out = y @ w_proj + b_proj
            return (out, attn_matrix)
        key = jax.random.key(seed)
        k1, k2, k3 = jax.random.split(key, 3)
        B, N, C = (64, 256, 192)
        x = jax.random.normal(k1, (B, N, C), dtype=jnp.float32)
        w_qkv = jax.random.normal(k2, (C, 3 * C), dtype=jnp.float32) * 0.02
        w_proj = jax.random.normal(k3, (C, C), dtype=jnp.float32) * 0.02
        b_proj = jnp.zeros((C,), dtype=jnp.float32)
        return {'x': x, 'w_qkv': w_qkv, 'w_proj': w_proj, 'b_proj': b_proj}
    _L0_attn_all = _L0_attn_setup()
    _L0_attn_in = {k: v for k, v in _L0_attn_all.items() if k in ('w_qkv', 'w_proj', 'b_proj')}
    del _L0_attn_all

    def _L0_ffn_setup():
        import jax, jax.numpy as jnp
        import numpy as np
        N_EMBD = 192
        FULL_SIZE = 16 * N_EMBD
        K = 4 * N_EMBD
        B, T = (8, 256)

        def _topk_mask(ck, k):
            probs = jax.nn.softmax(ck, axis=-1)
            _, idx = jax.lax.top_k(probs, k)
            b = jnp.arange(probs.shape[0])[:, None]
            return jnp.zeros_like(probs).at[b, idx].set(1.0)
        key = jax.random.key(seed)
        k0, k1, k2, k3, k4 = jax.random.split(key, 5)
        s = lambda fan_in: 1.0 / np.sqrt(fan_in)
        return {'x': jax.random.normal(k0, (B, T, N_EMBD), dtype=jnp.float32), 'w1': jax.random.normal(k1, (N_EMBD // 16, N_EMBD), dtype=jnp.float32) * s(N_EMBD), 'w2': jax.random.normal(k2, (FULL_SIZE, N_EMBD // 16), dtype=jnp.float32) * s(N_EMBD // 16), 'w_mfc': jax.random.normal(k3, (FULL_SIZE, N_EMBD), dtype=jnp.float32) * s(N_EMBD), 'w_proj': jax.random.normal(k4, (N_EMBD, FULL_SIZE), dtype=jnp.float32) * s(FULL_SIZE)}
    _L0_ffn_all = _L0_ffn_setup()
    _L0_ffn_in = {k: v for k, v in _L0_ffn_all.items() if k in ('w1', 'w2', 'w_mfc', 'w_proj')}
    del _L0_ffn_all
    return {'x': x, 'L0_tok_w_proj': _L0_tok_in['w_proj'], 'L0_tok_b_proj': _L0_tok_in['b_proj'], 'L0_tok_ln_gamma': _L0_tok_in['ln_gamma'], 'L0_tok_ln_beta': _L0_tok_in['ln_beta'], 'L0_attn_w_qkv': _L0_attn_in['w_qkv'], 'L0_attn_w_proj': _L0_attn_in['w_proj'], 'L0_attn_b_proj': _L0_attn_in['b_proj'], 'L0_ffn_w1': _L0_ffn_in['w1'], 'L0_ffn_w2': _L0_ffn_in['w2'], 'L0_ffn_w_mfc': _L0_ffn_in['w_mfc'], 'L0_ffn_w_proj': _L0_ffn_in['w_proj']}

def reference(x, L0_tok_w_proj, L0_tok_b_proj, L0_tok_ln_gamma, L0_tok_ln_beta, L0_attn_w_qkv, L0_attn_w_proj, L0_attn_b_proj, L0_ffn_w1, L0_ffn_w2, L0_ffn_w_mfc, L0_ffn_w_proj):
    import jax
    import jax.numpy as jnp

    def _L0_tok_ref(x, w_proj, b_proj, ln_gamma, ln_beta):
        import jax, jax.numpy as jnp
        import numpy as np
        IMG = 224
        PATCH = 16
        C_IN = 3
        EMBED = 192
        PATCH_DIM = C_IN * PATCH * PATCH
        BATCH = 64

        def _layernorm(h, gamma, beta, eps=1e-05):
            mu = jnp.mean(h, axis=-1, keepdims=True)
            var = jnp.mean(jnp.square(h - mu), axis=-1, keepdims=True)
            return (h - mu) * jax.lax.rsqrt(var + eps) * gamma + beta
        B, C, H, W = x.shape
        ph, pw = (H // PATCH, W // PATCH)
        p = x.reshape(B, C, ph, PATCH, pw, PATCH)
        p = jnp.transpose(p, (0, 2, 4, 1, 3, 5)).reshape(B, ph * pw, PATCH_DIM)
        h = jnp.einsum('bnd,de->bne', p, w_proj) + b_proj
        return _layernorm(h, ln_gamma, ln_beta)

    def _L0_attn_ref(x, w_qkv, w_proj, b_proj):
        import jax, jax.numpy as jnp
        import numpy as np
        NUM_HEADS = 12

        def _l2_norm(t):
            return t / jnp.linalg.norm(t, axis=-2, keepdims=True)

        def _reference_tuple_inner(x, w_qkv, w_proj, b_proj):
            B, N, C = x.shape
            H = NUM_HEADS
            D = C // H
            qkv = (x @ w_qkv).reshape(B, N, 3, H, D).transpose(2, 0, 3, 1, 4)
            q, k, v = (qkv[0], qkv[1], qkv[2])
            q = _l2_norm(q)
            kT = _l2_norm(k).transpose(0, 1, 3, 2)
            sum_k = kT.sum(axis=-1)
            D_inv = 1.0 / (N + jnp.einsum('bhnd,bhd->bhd', q, sum_k))
            attn_matrix = jnp.einsum('bhnd,bhdn->bhdn', q, kT) * D_inv[..., None]
            matrix = jnp.einsum('bhnd,bhdn->bdhn', v, kT)
            y = jnp.einsum('bdhn,bhdn->bhnd', matrix, attn_matrix)
            y = y.transpose(0, 2, 1, 3).reshape(B, N, C)
            out = y @ w_proj + b_proj
            return (out, attn_matrix)
        return _reference_tuple_inner(x, w_qkv, w_proj, b_proj)[0]

    def _L0_ffn_ref(x, w1, w2, w_mfc, w_proj):
        import jax, jax.numpy as jnp
        import numpy as np
        N_EMBD = 192
        FULL_SIZE = 16 * N_EMBD
        K = 4 * N_EMBD
        B, T = (8, 256)

        def _topk_mask(ck, k):
            probs = jax.nn.softmax(ck, axis=-1)
            _, idx = jax.lax.top_k(probs, k)
            b = jnp.arange(probs.shape[0])[:, None]
            return jnp.zeros_like(probs).at[b, idx].set(1.0)
        pooled = x.mean(axis=1)
        ck = jax.nn.relu(pooled @ w1.T) @ w2.T
        mask = _topk_mask(ck, K)
        h = jnp.einsum('btd,fd->btf', x, w_mfc) * mask[:, None, :]
        h = jax.nn.relu(h)
        out = jnp.einsum('btf,ef->bte', h, w_proj)
        return out
    h = _L0_tok_ref(x, L0_tok_w_proj, L0_tok_b_proj, L0_tok_ln_gamma, L0_tok_ln_beta)
    h = h + _L0_attn_ref(_layernorm(h, axis=-1), L0_attn_w_qkv, L0_attn_w_proj, L0_attn_b_proj)
    h = h + _L0_ffn_ref(_layernorm(h, axis=-1), L0_ffn_w1, L0_ffn_w2, L0_ffn_w_mfc, L0_ffn_w_proj)
    return h

_drawn_inputs = setup_inputs


def setup_inputs(seed=0):
    import zlib

    import numpy as np

    out = dict(_drawn_inputs(seed))
    spreads = {'L0_tok_b_proj': (0.0, 0.1),
     'L0_tok_ln_gamma': (1.0, 0.2),
     'L0_tok_ln_beta': (0.0, 0.1),
     'L0_attn_b_proj': (0.0, 0.1)}
    factors = {}
    for name, (base, spread) in spreads.items():
        noise = np.random.default_rng([zlib.crc32(name.encode()), seed]).standard_normal(out[name].shape)
        drawn = base * np.exp(spread * noise) if base else spread * noise
        out[name] = jnp.asarray(drawn.astype(out[name].dtype))
    for name, factor in factors.items():
        out[name] = (out[name] * factor).astype(out[name].dtype)
    return out
```

```python
from contextlib import ExitStack

import concourse.bass as bass
from concourse import mybir

F32 = mybir.dt.float32
BF16 = mybir.dt.bfloat16
I32 = mybir.dt.int32
U32 = mybir.dt.uint32
ALU = mybir.AluOpType
ACT = mybir.ActivationFunctionType
AX_X = mybir.AxisListType.X

P = 128
EPS = 1e-5
EXP_UNDERFLOW = 87.336544


def vit_tower(nc, x, w_tok, b_tok, gamma, beta, w_qkv, w_attn, b_attn, w1, w2, w_mfc, w_ffn, out):
    B, C_IN, IMG, _ = x.shape
    PATCH = 16
    G = IMG // PATCH
    N = G * G
    HALF = N // 2
    E = w_tok.shape[1]
    EB = E - P
    F = w_mfc.shape[0]
    R = w1.shape[0]
    K = 4 * E
    ROWS = C_IN * PATCH
    ODD = 64
    KX = ODD + ROWS
    JH = PATCH // 2
    SLOTS = K // P
    FH = F // 2
    NCH = FH // P
    NG = 2 * NCH
    LO = 32
    HI = K // LO
    UN = 4
    BANK = 512
    assert N % 2 == 0 and K % (P * LO // 32) == 0 and B % UN == 0 and 2 * B == P and HALF <= P

    table = nc.dram_tensor("ffn_table", (F, 2 * E), F32, kind="Internal").ap()
    tok_rows = w_tok.rearrange("(r j) e -> r j e", j=PATCH)
    out_rows = out.rearrange("b (h t) e -> b t h e", h=2)

    ctx = ExitStack()
    with ctx:
        def sb(name, shape, dt=F32):
            return ctx.enter_context(nc.sbuf_tensor(name, shape, dt))

        def sem(name):
            return ctx.enter_context(nc.semaphore(name))

        resid = sb("resid", [P, 2 * B, E])
        arena = sb("arena", [P, UN * SLOTS * 2 * E])
        patches = [arena[:, p * N * PATCH:(p + 1) * N * PATCH].rearrange("p (t j) -> p t j", j=PATCH)
                   for p in range(2)]
        row = [arena[:, s * FH:(s + 1) * FH] for s in range(6)]
        w2T = arena[0:R, 4 * FH:6 * FH]
        gathered = [arena[:, g * SLOTS * 2 * E:(g + 1) * SLOTS * 2 * E].rearrange("p (s e) -> p s e", s=SLOTS)
                    for g in range(UN)]
        wtok = sb("wtok", [P, JH, E])
        wq_a = sb("wq_a", [P, 3 * E])
        wq_b = sb("wq_b", [EB, 3 * E])
        wp_a = sb("wp_a", [P, E])
        wp_b = sb("wp_b", [EB + 1, E])
        gam = sb("gam", [P, 2, E])
        bet = sb("bet", [P, 2, E])
        ident = sb("ident", [P, P])
        pair = sb("pair", [P, P])
        swap = sb("swap", [P, P])
        lower = sb("lower", [P, P])
        mean_col = sb("mean_col", [P, 1])
        eps = sb("eps", [P, 1])
        stats = sb("stats", [P, 3, 2, 6])
        mv = sb("mv", [P, 3, 2, 2])
        sd = sb("sd", [P, 3, 2])
        rs = sb("rs", [P, 2, 2])
        z1 = sb("z1", [P, 2, E])
        z2 = sb("z2", [P, 2, E])
        hn = sb("hn", [P, 2, E])
        hn2 = sb("hn2", [P, 2, E])
        hnT_a = sb("hnT_a", [P, N])
        hnT_b = sb("hnT_b", [EB, N])
        ffn_mean = sb("ffn_mean", [P, 2 * B])
        ffn_rstd = sb("ffn_rstd", [P, 2 * B])
        q_s = sb("q_s", [P, 2, N])
        k2 = sb("k2", [P, 2, N])
        kb_s = sb("kb_s", [EB, N])
        act_junk = sb("act_junk", [P, 3, N])
        vq = sb("vq", [P, 2, N])
        sums = sb("sums", [P, 2, 2])
        squares = sb("squares", [P, 2, 2])
        roots_in = sb("roots_in", [P, 2])
        roots = sb("roots", [P, 2, 2])
        sqsk = sb("sqsk", [P, 2])
        denom = sb("denom", [P, 2, 2])
        coef = sb("coef", [P, 2])
        yT_a = sb("yT_a", [P, N])
        yT_b = sb("yT_b", [EB + 1, N])
        pooled_a = sb("pooled_a", [P, B])
        pooled_b = sb("pooled_b", [EB, B])
        w1T_a = sb("w1T_a", [P, R])
        w1T_b = sb("w1T_b", [EB, R])
        w2_rows = sb("w2_rows", [P, NG, R])
        router = sb("router", [R, B])
        top = sb("top", [P, 1])
        top_both = sb("top_both", [P, 1])
        count = sb("count", [P, 1])
        lt_count = sb("lt_count", [P, 1])
        eq_count = sb("eq_count", [P, 1])
        ties_left = sb("ties_left", [P, 1])
        ties_before = sb("ties_before", [P, 1])
        chosen_count = sb("chosen_count", [P, 1])
        chosen_before = sb("chosen_before", [P, 1])
        bit = sb("bit", [P, 1], I32)
        bound = sb("bound", [P, 1], I32)
        trial = sb("trial", [P, 1], I32)
        kept_bit = sb("kept_bit", [P, 1], I32)
        lo_T = sb("lo_T", [P, NG, B], I32)
        hi_T = sb("hi_T", [P, NG, B], I32)
        iota32 = sb("iota32", [P, LO], I32)
        group_no = sb("group_no", [P, NG], BF16)
        feature_no = sb("feature_no", [P, 1])
        wf_a = sb("wf_a", [P, 2, P])
        wf_b = sb("wf_b", [EB, 2, P])
        wfT = sb("wfT", [P, 2, E])
        onehot_lo = sb("onehot_lo", [P, NG, LO], BF16)
        onehot_hi = sb("onehot_hi", [P, NG, HI], BF16)
        hi_vals = sb("hi_vals", [P, NG, 2, HI], BF16)
        groups_f = sb("groups_f", [LO, HI])
        index = [sb(f"index{p}", [P, SLOTS], U32) for p in range(2)]
        wT_a = sb("wT_a", [P, K])
        wT_b = sb("wT_b", [EB, K])
        hidden = sb("hidden", [P, SLOTS, N])
        final = sb("final", [P, 2, 2, E])
        ps = ctx.enter_context(nc.psum_tensor("ps", [P, 8, BANK], F32))
        EMB, TRN, QK_A, V_AB, QK_B, PRJ, POOLED = (0, 1), 2, 3, 4, 5, 6, 7
        ROUTER, CROSS, TAB = 6, 7, (3, 4)
        UP, WT, FNT, DOWN, LIST = (0, 1), (2, 3), 4, (5, 6), 7

        pads_set = sem("pads_set")
        fills_set = sem("fills_set")
        const_step = sem("const_step")
        consts_set = sem("consts_set")
        weights_in = sem("weights_in")
        x_in = [sem(f"x_in{p}") for p in range(2)]
        x_ready = sem("x_ready")
        embed_done = sem("embed_done")
        ln_stats = [sem(f"ln{k}_stats") for k in range(3)]
        ln_mv = [sem(f"ln{k}_mv") for k in range(3)]
        ln_sd = [sem(f"ln{k}_sd") for k in range(3)]
        ln_rs = [sem(f"ln{k}_rs") for k in range(3)]
        z1_ready = sem("z1_ready")
        z2_ready = sem("z2_ready")
        h1_ready = sem("h1_ready")
        hn_ready = sem("hn_ready")
        hnT_done = sem("hnT_done")
        hnT_ready = sem("hnT_ready")
        qkv_done = sem("qkv_done")
        kb_ready = sem("kb_ready")
        sums_ready = sem("sums_ready")
        squares_ready = sem("squares_ready")
        roots_in_ready = sem("roots_in_ready")
        roots_ready = sem("roots_ready")
        sqsk_ready = sem("sqsk_ready")
        denom0_ready = sem("denom0_ready")
        denom_ready = sem("denom_ready")
        coef_ready = sem("coef_ready")
        vq_ready = sem("vq_ready")
        y_ready = sem("y_ready")
        proj_done = sem("proj_done")
        resid_ready = sem("resid_ready")
        hn2_ready = sem("hn2_ready")
        pool_done = sem("pool_done")
        pool_kept = sem("pool_kept")
        w2T_done = sem("w2T_done")
        w2T_ready = sem("w2T_ready")
        router_done = sem("router_done")
        router_ready = sem("router_ready")
        scores_done = sem("scores_done")
        sel_step = sem("sel_step")
        cross_done = sem("cross_done")
        trial_ready = sem("trial_ready")
        count_ready = sem("count_ready")
        total_done = sem("total_done")
        kept_ready = sem("kept_ready")
        bound_ready = sem("bound_ready")
        bit_ready = sem("bit_ready")
        wf_in = [sem(f"wf_in{p}") for p in range(2)]
        wfT_done = sem("wfT_done")
        wfT_ready = sem("wfT_ready")
        tab_out = [sem(f"tab_out{p}") for p in range(2)]
        mfc_out = sem("mfc_out")
        slotT_done = sem("slotT_done")
        lohi_ready = sem("lohi_ready")
        onehot_ready = sem("onehot_ready")
        hi_vals_ready = sem("hi_vals_ready")
        list_done = sem("list_done")
        groups_f_ready = sem("groups_f_ready")
        index_ready = sem("index_ready")
        rows_in = [sem(f"rows_in{g}") for g in range(UN)]
        fn_ready = sem("fn_ready")
        fnT_done = sem("fnT_done")
        fnT_ready = sem("fnT_ready")
        wT_done = sem("wT_done")
        wT_vec = sem("wT_vec")
        wT_act = sem("wT_act")
        up_done = sem("up_done")
        hid_ready = sem("hid_ready")
        down_done = sem("down_done")
        final_ready = sem("final_ready")
        vector_passed = sem("vector_passed")
        pool_passed = sem("pool_passed")
        stored = [sem(f"stored{p}") for p in range(2)]

        N_WEIGHTS = 17
        LAG1 = 3
        LAG2 = 3
        BITS = 31
        PLAIN_BITS = BITS - NG

        def over_images(eng, unroll, lag, body):
            for n in range(2 * unroll):
                body(n, n % unroll, lambda k, n=n: 0 <= n - k < B)
            with eng.Fori(2, B // unroll) as i:
                for q in range(unroll):
                    body(unroll * i + q, q, lambda k: True)
            for n in range(B, B + lag):
                body(n, n % unroll, lambda k, n=n: 0 <= n - k < B)

        def at_least(eng, s, value):
            if not isinstance(value, int) or value > 0:
                eng.wait_ge(s, value)

        def image(m):
            return resid[0:HALF, bass.ds(2 * m, 2), :]

        block = ctx.enter_context(nc.Block())

        @block.sync
        def _(sp):
            gamma_row = gamma.rearrange("(a e) -> a e", a=1)
            beta_row = beta.rearrange("(a e) -> a e", a=1)
            loads = [
                (wtok[0:ROWS, :, :], tok_rows[:, 0:JH, :]),
                (wtok[ODD:KX, :, :], tok_rows[:, JH:PATCH, :]),
                (wtok[ROWS:ROWS + 1, 0, :], b_tok.rearrange("(a e) -> a e", a=1)),
            ]
            loads += [(t[0:HALF, h, :], r.to_broadcast([HALF, E]))
                      for t, r in ((gam, gamma_row), (bet, beta_row)) for h in range(2)]
            for rows, dst in ((slice(0, P), wq_a), (slice(P, E), wq_b)):
                three = w_qkv[rows, :].rearrange("c (m e) -> c m e", m=3)
                loads.append((dst[:, 0:3 * P].rearrange("c (m e) -> c m e", m=3), three[:, :, 0:P]))
                loads.append((dst[:, 3 * P:3 * E].rearrange("c (m e) -> c m e", m=3), three[:, :, P:E]))
            loads += [
                (wp_a[:, :], w_attn[0:P, :]),
                (wp_b[0:EB, :], w_attn[P:E, :]),
                (wp_b[EB:EB + 1, :], b_attn.rearrange("(a e) -> a e", a=1)),
                (w1T_a[:, :], w1.rearrange("r c -> c r")[0:P, :]),
                (w1T_b[:, :], w1.rearrange("r c -> c r")[P:E, :]),
                (w2_rows[:, :, :], w2.rearrange("(g p) r -> p g r", p=P)),
            ]
            assert len(loads) == N_WEIGHTS

            def load_x(n, p):
                at_least(sp, embed_done, n - 1)
                for c in range(C_IN):
                    src = x[bass.ds(n, 1), c, :, :].rearrange("b (g k) w -> k (b g) w", k=PATCH)
                    dst = patches[p][c * PATCH:(c + 1) * PATCH, :, :].rearrange("k (g t) j -> k g (t j)", g=G)
                    sp.dma_start(dst, src).then_inc(x_in[p], 16)

            sp.wait_ge(pads_set, 1)
            load_x(0, 0)
            for dst, src in loads[:3]:
                sp.dma_start(dst, src).then_inc(weights_in, 16)
            load_x(1, 1)
            with nc.allow_non_contiguous_dma(reason="w1 comes in transposed: 2304 words"):
                for dst, src in loads[3:]:
                    sp.dma_start(dst, src).then_inc(weights_in, 16)
            sp.dma_start(table[:, 0:E], w_mfc).then_inc(mfc_out, 16)
            with sp.Fori(1, B // 2) as i:
                for p in range(2):
                    load_x(2 * i + p, p)

            def load_wf(c, p):
                at_least(sp, wfT_done, c - 1)
                cols = bass.ds(c * P, P)
                sp.dma_start(wf_a[:, p, :], w_ffn[0:P, cols]).then_inc(wf_in[p], 16)
                sp.dma_start(wf_b[:, p, :], w_ffn[P:E, cols]).then_inc(wf_in[p], 16)

            def store_wf(c, p):
                sp.wait_ge(wfT_ready, c + 1)
                sp.dma_start(table[bass.ds(c * P, P), E:2 * E], wfT[:, p, :]).then_inc(tab_out[p], 16)

            load_wf(0, 0)
            load_wf(1, 1)
            with sp.Fori(0, NG // 2 - 1) as i:
                for p in range(2):
                    store_wf(2 * i + p, p)
                    load_wf(2 * i + 2 + p, p)
            for p in range(2):
                store_wf(NG - 2 + p, p)

            def store(m, p):
                sp.wait_ge(final_ready, m + 1)
                sp.dma_start(out_rows[bass.ds(m, 1), :, :, :].rearrange("b t h e -> (b t) h e"),
                             final[0:HALF, p, :, :]).then_inc(stored[p], 16)

            with sp.Fori(0, B // 2) as i:
                for p in range(2):
                    store(2 * i + p, p)
            for p in range(2):
                sp.wait_ge(stored[p], 16 * (B // 2))

        @block.gpsimd
        def _(pool):
            pool.iota(iota32[:, :], [[1, LO]], base=0, channel_multiplier=0)
            pool.iota(group_no[:, :], [[1, NCH], [NCH, 2]], base=0, channel_multiplier=0,
                      allow_small_or_imprecise_dtypes=True)
            pool.iota(feature_no[:, :], [[1, 1]], base=0, channel_multiplier=1,
                      allow_small_or_imprecise_dtypes=True)
            for m in (ident, pair, swap, lower):
                last = pool.memset(m[:, :], 0.0)
            last.then_inc(const_step, 1)
            turns = [(ident, 0), (pair, 0), (swap, B), (lower, B), (pair, B), (swap, -B), (pair, -B)]
            for k, (m, offset) in enumerate(turns):
                pool.wait_ge(const_step, k + 1)
                last = pool.affine_select(out=m[:, :], in_=m[:, :], compare_op=ALU.not_equal, fill=1.0,
                                          base=offset, pattern=[[-1, P]], channel_multiplier=1)
                last.then_inc(const_step if k + 1 < len(turns) else consts_set, 1)

            pool.wait_ge(weights_in, 16 * N_WEIGHTS)

            def affine(m):
                pool.wait_ge(z1_ready, m + 1)
                at_least(pool, h1_ready, m)
                pool.tensor_tensor(z2[0:HALF, :, :], z1[0:HALF, :, :], gam[0:HALF, :, :],
                                   ALU.mult).then_inc(z2_ready, 1)
                pool.wait_ge(z2_ready, m + 1)
                pool.tensor_tensor(image(m), z2[0:HALF, :, :], bet[0:HALF, :, :],
                                   ALU.add).then_inc(h1_ready, 1)

            affine(0)
            with pool.Fori(1, B) as i:
                affine(i)

            for p in range(2):
                pool.wait_ge(tab_out[p], 16 * (NG // 2))
            pool.wait_ge(mfc_out, 16)

            def list_values(m):
                pool.wait_ge(onehot_ready, 2 * m + 1)
                at_least(pool, list_done, m)
                pool.tensor_tensor(hi_vals[:, :, 0, :], onehot_hi[:, :, :],
                                   group_no[:, :].unsqueeze(2).to_broadcast([P, NG, HI]), ALU.mult)
                pool.tensor_scalar(hi_vals[:, :, 1, :], onehot_hi[:, :, :], feature_no[:, :], None,
                                   ALU.mult).then_inc(hi_vals_ready, 1)

            def gather(m, g):
                pool.wait_ge(index_ready, m + 1)
                at_least(pool, down_done, m - UN + 1)
                pool.sem_inc(pool_passed)
                for s in range(SLOTS):
                    pool.indirect_dma_start(
                        gathered[g][:, s, :], None, table,
                        bass.IndirectOffsetOnAxis(index[g % 2][:, s:s + 1], 0)).then_inc(rows_in[g], 16)

            def step(n, q, on):
                if on(0):
                    list_values(n)
                if on(1):
                    gather(n - 1, (q - 1) % UN)

            over_images(pool, UN, 1, step)

        @block.scalar
        def _(act):
            def sqrt_of_var(k, m):
                act.wait_ge(ln_mv[k], m + 1)
                at_least(act, ln_rs[k], m)
                nc.scalar.activation(sd[0:HALF, k, :], mv[0:HALF, k, :, 1], ACT.Sqrt,
                                     bias=eps[0:HALF, :]).then_inc(ln_sd[k], 1)

            def odd_half(n, p):
                act.wait_ge(x_in[p], 16 * C_IN * (n // 2 + 1) if isinstance(n, int) else (n - p) * (8 * C_IN) + 16 * C_IN)
                nc.scalar.activation(patches[p][ODD:KX, :, 0:JH], patches[p][0:ROWS, :, JH:PATCH],
                                     ACT.Copy).then_inc(x_ready, 1)

            def copy_hnT(m):
                act.wait_ge(hnT_done, m + 1)
                at_least(act, qkv_done, m)
                nc.scalar.activation(hnT_a[:, :], ps[:, TRN, 0:N], ACT.Copy)
                nc.scalar.activation(hnT_b[:, :], ps[0:EB, TRN, 256:256 + N], ACT.Copy).then_inc(hnT_ready, 1)

            def attention_sums(m):
                act.wait_ge(qkv_done, m + 1)
                at_least(act, y_ready, m)
                nc.scalar.activation(q_s[:, 0, :], ps[:, QK_A, 0:N], ACT.Identity, accum_out=sums[:, 0, 0:1])
                nc.scalar.activation(q_s[0:EB, 1, :], ps[0:EB, QK_B, 0:N], ACT.Identity,
                                     accum_out=sums[0:EB, 0, 1:2])
                nc.scalar.activation(act_junk[:, 0, :], ps[:, QK_A, N:2 * N], ACT.Identity,
                                     accum_out=sums[:, 1, 0:1]).then_inc(sums_ready, 1)
                nc.scalar.activation(act_junk[:, 1, :], ps[:, QK_A, 0:N], ACT.Square, accum_out=squares[:, 0, 0:1])
                nc.scalar.activation(act_junk[0:EB, 2, :], ps[0:EB, QK_B, 0:N], ACT.Square,
                                     accum_out=squares[0:EB, 0, 1:2])
                nc.scalar.activation(k2[:, 0, :], ps[:, QK_A, N:2 * N], ACT.Square, accum_out=squares[:, 1, 0:1])
                act.wait_ge(kb_ready, m + 1)
                nc.scalar.activation(k2[0:EB, 1, :], kb_s[:, :], ACT.Square,
                                     accum_out=squares[0:EB, 1, 1:2]).then_inc(squares_ready, 1)

            def attention_roots(m):
                act.wait_ge(roots_in_ready, m + 1)
                act.wait_ge(squares_ready, m + 1)
                nc.scalar.activation(roots[:, 0, :], roots_in[:, :], ACT.Sqrt)
                nc.scalar.activation(roots[:, 1, :], squares[:, 1, :], ACT.Sqrt).then_inc(roots_ready, 1)

            act.wait_ge(fills_set, 1)

            def step1(n, p, on):
                if on(3):
                    sqrt_of_var(2, n - 3)
                if on(0):
                    odd_half(n, p)
                if on(1):
                    sqrt_of_var(0, n - 1)
                if on(2):
                    attention_sums(n - 2)
                    attention_roots(n - 2)
                if on(1):
                    sqrt_of_var(1, n - 1)
                    copy_hnT(n - 1)

            over_images(act, 2, LAG1, step1)

            act.wait_ge(w2T_done, 1)
            for c in range(F // BANK):
                last = nc.scalar.activation(w2T[:, c * BANK:(c + 1) * BANK], ps[0:R, c, :], ACT.Copy)
            last.then_inc(w2T_ready, 1)
            act.wait_ge(router_done, 1)
            nc.scalar.activation(router[:, :], ps[0:R, ROUTER, 0:B], ACT.Relu).then_inc(router_ready, 1)

            def copy_wfT(c, p):
                act.wait_ge(wfT_done, c + 1)
                if not isinstance(c, int) or c >= 2:
                    act.wait_ge(tab_out[p], (c - p) * 8)
                nc.scalar.activation(wfT[:, p, :], ps[:, TAB[p], 0:E], ACT.Copy).then_inc(wfT_ready, 1)

            for c in range(2):
                copy_wfT(c, c)
            with act.Fori(1, NG // 2) as i:
                for p in range(2):
                    copy_wfT(2 * i + p, p)

            def copy_fnT(m):
                act.wait_ge(fnT_done, m + 1)
                at_least(act, up_done, 3 * m)
                nc.scalar.activation(hnT_a[:, :], ps[:, FNT, 0:N], ACT.Copy)
                nc.scalar.activation(hnT_b[:, :], ps[0:EB, FNT, 256:256 + N], ACT.Copy).then_inc(fnT_ready, 1)

            def copy_wT(m):
                act.wait_ge(wT_done, 3 * m + 2)
                at_least(act, up_done, 3 * m)
                nc.scalar.activation(wT_a[:, 2 * P:4 * P], ps[:, WT[1], 0:2 * P], ACT.Copy)
                nc.scalar.activation(wT_b[:, 2 * P:4 * P], ps[0:EB, WT[1], 2 * P:4 * P],
                                     ACT.Copy).then_inc(wT_act, 1)

            def relu(m):
                at_least(act, down_done, m)
                for s in range(3):
                    act.wait_ge(up_done, 3 * m + s + 1)
                    nc.scalar.activation(hidden[:, 2 * s:2 * s + 2, :].rearrange("p s t -> p (s t)"),
                                         ps[:, UP[s % 2], 0:2 * N], ACT.Relu).then_inc(hid_ready, 1)

            def step2(n, q, on):
                if on(3):
                    relu(n - 3)
                if on(2):
                    copy_fnT(n - 2)
                    copy_wT(n - 2)

            over_images(act, UN, LAG2, step2)

        @block.vector
        def _(dve):
            nc.vector.memset(patches[0][32:64, :, :], 1.0)
            nc.vector.memset(patches[1][32:64, :, :], 1.0)
            nc.vector.memset(wtok[32:64, :, :], 0.0).then_inc(pads_set, 1)
            nc.vector.memset(eps[:, :], EPS)
            nc.vector.memset(mean_col[:, :], 1.0 / N)
            nc.vector.memset(yT_b[EB:EB + 1, :], 1.0)
            nc.vector.memset(sums[:, :, :], 1.0)
            nc.vector.memset(squares[:, :, :], 1.0)
            nc.vector.memset(bit[:, :], 1 << (BITS - 1))
            nc.vector.memset(bound[:, :], 0).then_inc(fills_set, 1)

            def apart():
                dve.sem_inc(vector_passed)

            def normalise(k, m, source, waits, out_tile, out_ready, free):
                for s, v in waits:
                    dve.wait_ge(s, v)
                apart()
                for h in range(2):
                    last = nc.vector.bn_stats(stats[0:HALF, k, h, :], source(h))
                last.then_inc(ln_stats[k], 1)
                dve.wait_ge(ln_stats[k], m + 1)
                apart()
                for h in range(2):
                    last = nc.vector.bn_aggr(mv[0:HALF, k, h, :], stats[0:HALF, k, h, :])
                last.then_inc(ln_mv[k], 1)
                dve.wait_ge(ln_sd[k], m + 1)
                rstd = rs[0:HALF, k, :] if k < 2 else ffn_rstd[0:HALF, bass.ds(2 * m, 2)]
                nc.vector.reciprocal(rstd, sd[0:HALF, k, :]).then_inc(ln_rs[k], 1)
                dve.wait_ge(ln_rs[k], m + 1)
                at_least(dve, free, m)
                for h in range(2):
                    r = rs[0:HALF, k, h:h + 1] if k < 2 else ffn_rstd[0:HALF, bass.ds(2 * m + h, 1)]
                    last = nc.vector.tensor_scalar(out_tile[0:HALF, h, :], source(h), mv[0:HALF, k, h, 0:1], r,
                                                   ALU.subtract, ALU.mult)
                last.then_inc(out_ready, 1)

            def ln0(m, p):
                normalise(0, m, lambda h: ps[0:HALF, EMB[p], h * E:(h + 1) * E], [(embed_done, m + 1)],
                          z1, z1_ready, z2_ready)

            def ln1(m):
                normalise(1, m, lambda h: image(m)[:, h, :], [(h1_ready, m + 1)], hn, hn_ready, hnT_done)

            def attention(m):
                dve.wait_ge(qkv_done, m + 1)
                nc.vector.tensor_copy(kb_s[:, :], ps[EB:2 * EB, QK_B, 0:N]).then_inc(kb_ready, 1)
                dve.wait_ge(kb_ready, m + 1)
                nc.vector.tensor_reduce(sums[0:EB, 1, 1:2], kb_s[:, :], AX_X, ALU.add)
                dve.wait_ge(sums_ready, m + 1)
                nc.vector.tensor_tensor(vq[:, 0, :], ps[:, V_AB, 0:N], q_s[:, 0, :], ALU.mult)
                nc.vector.tensor_tensor(vq[0:EB, 1, :], ps[0:EB, V_AB, N:2 * N], q_s[0:EB, 1, :],
                                        ALU.mult).then_inc(vq_ready, 1)
                dve.wait_ge(vq_ready, m + 1)
                nc.vector.tensor_tensor(sqsk[:, :], sums[:, 0, :], sums[:, 1, :], ALU.mult).then_inc(sqsk_ready, 1)
                dve.wait_ge(squares_ready, m + 1)
                nc.vector.tensor_tensor(roots_in[:, :], squares[:, 0, :], squares[:, 1, :],
                                        ALU.mult).then_inc(roots_in_ready, 1)
                dve.wait_ge(roots_ready, m + 1)
                dve.wait_ge(sqsk_ready, m + 1)
                nc.vector.scalar_tensor_tensor(out=denom[:, 0, :], in0=roots[:, 0, :], scalar=float(N),
                                               in1=sqsk[:, :], op0=ALU.mult,
                                               op1=ALU.add).then_inc(denom0_ready, 1)
                dve.wait_ge(denom0_ready, m + 1)
                nc.vector.tensor_tensor(denom[:, 1, :], denom[:, 0, :], roots[:, 1, :],
                                        ALU.mult).then_inc(denom_ready, 1)
                dve.wait_ge(denom_ready, m + 1)
                nc.vector.reciprocal(coef[:, :], denom[:, 1, :]).then_inc(coef_ready, 1)
                dve.wait_ge(coef_ready, m + 1)
                at_least(dve, proj_done, m)
                nc.vector.scalar_tensor_tensor(out=yT_a[:, :], in0=vq[:, 0, :], scalar=coef[:, 0:1],
                                               in1=k2[:, 0, :], op0=ALU.mult, op1=ALU.mult)
                nc.vector.scalar_tensor_tensor(out=yT_b[0:EB, :], in0=vq[0:EB, 1, :], scalar=coef[0:EB, 1:2],
                                               in1=k2[0:EB, 1, :], op0=ALU.mult,
                                               op1=ALU.mult).then_inc(y_ready, 1)

            def residual_and_ln2(m):
                dve.wait_ge(proj_done, m + 1)
                dve.wait_ge(hn_ready, m + 1)
                nc.vector.tensor_tensor(image(m), ps[0:HALF, PRJ, 0:2 * E].rearrange("p (h e) -> p h e", h=2),
                                        image(m), ALU.add).then_inc(resid_ready, 1)
                normalise(2, m, lambda h: image(m)[:, h, :], [(resid_ready, m + 1)], hn2, hn2_ready, pool_done)
                nc.vector.tensor_copy(ffn_mean[0:HALF, bass.ds(2 * m, 2)], mv[0:HALF, 2, :, 0])

            def keep_pooled(m):
                dve.wait_ge(pool_done, m + 1)
                nc.vector.tensor_copy(pooled_a[:, bass.ds(m, 1)], ps[:, POOLED, 0:1])
                nc.vector.tensor_copy(pooled_b[:, bass.ds(m, 1)], ps[0:EB, POOLED, 1:2]).then_inc(pool_kept, 1)

            dve.wait_ge(fills_set, 1)
            dve.wait_ge(weights_in, 16 * N_WEIGHTS)

            def step1(n, p, on):
                if on(3):
                    residual_and_ln2(n - 3)
                if on(1):
                    ln0(n - 1, 1 - p)
                if on(2):
                    attention(n - 2)
                if on(1):
                    ln1(n - 1)
                if on(3):
                    keep_pooled(n - 3)

            over_images(dve, 2, LAG1, step1)

            done = 0

            def then(instruction):
                nonlocal done
                done += 1
                instruction.then_inc(sel_step, 1)
                dve.wait_ge(sel_step, done)

            scores = ps[:, 0:3, :].rearrange("p b c -> p (b c)")
            dist, below, tied, running, ones, slots = row[0], row[1], row[2], row[3], row[4], row[5]
            dve.wait_ge(scores_done, 1)
            nc.vector.memset(ones, 1.0)
            then(nc.vector.tensor_reduce(top[:, :], scores, AX_X, ALU.max))
            dve.wait_ge(cross_done, 1)
            then(nc.vector.tensor_tensor(top_both[:, :], ps[:, CROSS, 0:1], top[:, :], ALU.max))
            then(nc.vector.tensor_scalar(dist, scores, top_both[:, :], -1.0, ALU.subtract, ALU.mult))
            then(nc.vector.tensor_scalar(dist, dist, EXP_UNDERFLOW, None, ALU.min))

            def search_bit(b):
                at_least(dve, bound_ready, b)
                at_least(dve, bit_ready, b)
                nc.vector.tensor_tensor(trial[:, :], bound[:, :], bit[:, :], ALU.bitwise_or).then_inc(trial_ready, 1)
                dve.wait_ge(trial_ready, b + 1)
                nc.vector.tensor_scalar(below, dist, trial[:, :].bitcast(F32), 0.0, ALU.is_lt, ALU.add,
                                        accum_out=count[:, :]).then_inc(count_ready, 1)
                dve.wait_ge(total_done, b + 1)
                nc.vector.tensor_scalar(kept_bit[:, :], ps[:, CROSS, 0:1], K - 0.5, bit[:, :],
                                        ALU.is_lt, ALU.mult).then_inc(kept_ready, 1)
                dve.wait_ge(kept_ready, b + 1)
                nc.vector.tensor_tensor(bound[:, :], bound[:, :], kept_bit[:, :],
                                        ALU.bitwise_or).then_inc(bound_ready, 1)
                nc.vector.tensor_scalar(bit[:, :], bit[:, :], 1, None,
                                        ALU.logical_shift_right).then_inc(bit_ready, 1)

            search_bit(0)
            with dve.Fori(1, BITS) as b:
                search_bit(b)
            dve.wait_ge(bound_ready, BITS)

            kth = bound[:, :].bitcast(F32)
            nc.vector.tensor_scalar(below, dist, kth, 0.0, ALU.is_lt, ALU.add, accum_out=lt_count[:, :])
            then(nc.vector.tensor_scalar(tied, dist, kth, 0.0, ALU.is_equal, ALU.add, accum_out=eq_count[:, :]))
            dve.wait_ge(cross_done, 3)
            nc.vector.tensor_scalar(ties_left[:, :], ps[:, CROSS, 0:1], -1.0, float(K), ALU.mult, ALU.add)
            then(nc.vector.tensor_copy(ties_before[:, :], ps[:, CROSS, 1:2]))
            then(nc.vector.tensor_tensor_scan(running, ones, tied, ties_before[:, :], ALU.mult, ALU.add))
            then(nc.vector.scalar_tensor_tensor(out=tied, in0=running, scalar=ties_left[:, :], in1=tied,
                                                op0=ALU.is_le, op1=ALU.mult))
            then(nc.vector.scalar_tensor_tensor(out=below, in0=below, scalar=1.0, in1=tied, op0=ALU.mult,
                                                op1=ALU.add, accum_out=chosen_count[:, :]))
            dve.wait_ge(cross_done, 4)
            then(nc.vector.tensor_copy(chosen_before[:, :], ps[:, CROSS, 2:3]))
            then(nc.vector.tensor_tensor_scan(running, ones, below, chosen_before[:, :], ALU.mult, ALU.add))
            then(nc.vector.tensor_tensor(slots, running, below, ALU.mult))
            dve.wait_ge(slotT_done, 1)
            flat_hi = hi_T[:, :, :].rearrange("p g b -> p (g b)")
            flat_lo = lo_T[:, :, :].rearrange("p g b -> p (g b)")
            then(nc.vector.tensor_scalar(flat_hi, scores, -1.0, None, ALU.add))
            then(nc.vector.tensor_scalar(flat_lo, flat_hi, LO - 1, None, ALU.bitwise_and))
            nc.vector.tensor_scalar(flat_hi, flat_hi, LO.bit_length() - 1, None,
                                    ALU.arith_shift_right).then_inc(lohi_ready, 1)
            dve.wait_ge(lohi_ready, 1)

            def onehots(m):
                at_least(dve, list_done, m)
                at_least(dve, hi_vals_ready, m)
                values = iota32[:, :].unsqueeze(1)
                nc.vector.tensor_tensor(onehot_hi[:, :, :], hi_T[:, :, bass.ds(m, 1)].to_broadcast([P, NG, HI]),
                                        values[:, :, 0:HI].to_broadcast([P, NG, HI]),
                                        ALU.is_equal).then_inc(onehot_ready, 1)
                nc.vector.tensor_tensor(onehot_lo[:, :, :], lo_T[:, :, bass.ds(m, 1)].to_broadcast([P, NG, LO]),
                                        values.to_broadcast([P, NG, LO]), ALU.is_equal).then_inc(onehot_ready, 1)

            def write_index(m, q):
                dve.wait_ge(list_done, m + 1)
                at_least(dve, index_ready, m)
                nc.vector.tensor_scalar(groups_f[:, :], ps[0:LO, LIST, 0:HI], float(P), None,
                                        ALU.mult).then_inc(groups_f_ready, 1)
                dve.wait_ge(groups_f_ready, m + 1)
                g = (q - 2) % UN
                if isinstance(m, int):
                    at_least(dve, rows_in[g], 16 * SLOTS * ((m - 2) // UN + 1) if m >= 2 else 0)
                else:
                    dve.wait_ge(rows_in[g], (m - 2 - g) * (16 * SLOTS // UN) + 16 * SLOTS)
                for k in range(P // LO):
                    part = slice(k * SLOTS, (k + 1) * SLOTS)
                    last = nc.vector.tensor_tensor(index[q % 2][k * LO:(k + 1) * LO, :], groups_f[:, part],
                                                   ps[0:LO, LIST, HI + k * SLOTS:HI + (k + 1) * SLOTS], ALU.add)
                last.then_inc(index_ready, 1)

            def normalise_again(m):
                at_least(dve, fnT_done, m)
                for h in range(2):
                    last = nc.vector.tensor_scalar(hn2[0:HALF, h, :], image(m)[:, h, :],
                                                   ffn_mean[0:HALF, bass.ds(2 * m + h, 1)],
                                                   ffn_rstd[0:HALF, bass.ds(2 * m + h, 1)],
                                                   ALU.subtract, ALU.mult)
                last.then_inc(fn_ready, 1)

            def copy_wT(m):
                at_least(dve, up_done, 3 * m)
                for s in (0, 2):
                    dve.wait_ge(wT_done, 3 * m + s + 1)
                    cols = slice(2 * s * P, 2 * (s + 1) * P)
                    nc.vector.tensor_copy(wT_a[:, cols], ps[:, WT[0], 0:2 * P])
                    nc.vector.tensor_copy(wT_b[:, cols], ps[0:EB, WT[0], 2 * P:4 * P]).then_inc(wT_vec, 1)

            def add_residual(m, q):
                dve.wait_ge(down_done, m + 1)
                if isinstance(m, int):
                    at_least(dve, stored[q % 2], 16 * (m // 2))
                else:
                    dve.wait_ge(stored[q % 2], (m - q % 2) * 8)
                nc.vector.tensor_tensor(final[0:HALF, q % 2, :, :],
                                        ps[0:HALF, DOWN[q % 2], 0:2 * E].rearrange("p (h e) -> p h e", h=2),
                                        image(m), ALU.add).then_inc(final_ready, 1)

            def step2(n, q, on):
                if on(2):
                    normalise_again(n - 2)
                if on(0):
                    onehots(n)
                if on(2):
                    copy_wT(n - 2)
                if on(0):
                    write_index(n, q)
                if on(3):
                    add_residual(n - 3, (q - 3) % UN)

            over_images(dve, UN, LAG2, step2)

        @block.tensor
        def _(pe):
            pe.wait_ge(consts_set, 1)
            pe.wait_ge(fills_set, 1)
            pe.wait_ge(weights_in, 16 * N_WEIGHTS)

            def embed(n, p):
                pe.wait_ge(x_ready, n + 1)
                at_least(pe, z1_ready, n - 1)
                for h in range(2):
                    for j in range(JH):
                        last = nc.tensor.matmul(ps[0:HALF, EMB[p], h * E:(h + 1) * E],
                                                patches[p][0:KX, h * HALF:(h + 1) * HALF, j], wtok[0:KX, j, :],
                                                start=(j == 0), stop=(j == JH - 1))
                last.then_inc(embed_done, 1)

            def transpose_tokens(bank, source):
                for h in range(2):
                    nc.tensor.transpose(ps[:, bank, h * HALF:(h + 1) * HALF], source[0:HALF, h, 0:P],
                                        ident[0:HALF, 0:HALF])
                    last = nc.tensor.transpose(ps[0:EB, bank, 256 + h * HALF:256 + (h + 1) * HALF],
                                               source[0:HALF, h, P:E], ident[0:HALF, 0:HALF])
                return last

            def qkv(m):
                pe.wait_ge(hn_ready, m + 1)
                at_least(pe, hnT_ready, m)
                transpose_tokens(TRN, hn).then_inc(hnT_done, 1)
                pe.wait_ge(hnT_ready, m + 1)
                at_least(pe, y_ready, m)
                at_least(pe, squares_ready, m)
                for out_ap, first, width in (
                    (ps[:, QK_A, 0:N], 0, P), (ps[:, QK_A, N:2 * N], P, P),
                    (ps[:, V_AB, 0:N], 2 * P, P), (ps[0:EB, V_AB, N:2 * N], 3 * P + 2 * EB, EB),
                    (ps[:, QK_B, 0:N], 3 * P, 2 * EB),
                ):
                    nc.tensor.matmul(out_ap, wq_a[:, first:first + width], hnT_a[:, :], start=True, stop=False)
                    last = nc.tensor.matmul(out_ap, wq_b[:, first:first + width], hnT_b[:, :],
                                            start=False, stop=True)
                last.then_inc(qkv_done, 1)

            def project(m):
                pe.wait_ge(y_ready, m + 1)
                at_least(pe, resid_ready, m)
                for h in range(2):
                    o = ps[0:HALF, PRJ, h * E:(h + 1) * E]
                    half = slice(h * HALF, (h + 1) * HALF)
                    nc.tensor.matmul(o, yT_a[:, half], wp_a[:, :], start=True, stop=False)
                    last = nc.tensor.matmul(o, yT_b[:, half], wp_b[:, :], start=False, stop=True)
                last.then_inc(proj_done, 1)

            def pool_tokens(m):
                pe.wait_ge(hn2_ready, m + 1)
                at_least(pe, pool_kept, m)
                for o, chans in ((ps[:, POOLED, 0:1], slice(0, P)), (ps[0:EB, POOLED, 1:2], slice(P, E))):
                    for h in range(2):
                        last = nc.tensor.matmul(o, hn2[0:HALF, h, chans], mean_col[0:HALF, :],
                                                start=(h == 0), stop=(h == 1))
                last.then_inc(pool_done, 1)

            def step1(n, p, on):
                if on(0):
                    embed(n, p)
                if on(3):
                    pool_tokens(n - 3)
                if on(1):
                    qkv(n - 1)
                if on(2):
                    project(n - 2)

            over_images(pe, 2, LAG1, step1)

            pe.wait_ge(pool_kept, B)
            pe.wait_ge(resid_ready, B)
            pe.wait_ge(y_ready, B)
            for g in range(NG):
                last = nc.tensor.transpose(ps[0:R, g // 4, (g % 4) * P:(g % 4 + 1) * P], w2_rows[:, g, :],
                                           ident[:, :])
            last.then_inc(w2T_done, 1)
            nc.tensor.matmul(ps[0:R, ROUTER, 0:B], w1T_a[:, :], pooled_a[:, :], start=True, stop=False)
            nc.tensor.matmul(ps[0:R, ROUTER, 0:B], w1T_b[:, :], pooled_b[:, :], start=False,
                             stop=True).then_inc(router_done, 1)
            pe.wait_ge(w2T_ready, 1)
            pe.wait_ge(router_ready, 1)
            for h in range(2):
                for c in range(FH // BANK):
                    first = h * FH + c * BANK
                    last = nc.tensor.matmul(ps[h * B:(h + 1) * B, c, :], router[:, :],
                                            w2T[:, first:first + BANK], start=True, stop=True)
            last.then_inc(scores_done, 1)
            pe.wait_ge(sel_step, 1)
            nc.tensor.matmul(ps[:, CROSS, 0:1], swap[:, :], top[:, :], start=True, stop=True).then_inc(cross_done, 1)
            pe.wait_ge(sel_step, 2)

            def total(b):
                pe.wait_ge(count_ready, b + 1)
                at_least(pe, kept_ready, b)
                nc.tensor.matmul(ps[:, CROSS, 0:1], pair[:, :], count[:, :], start=True,
                                 stop=True).then_inc(total_done, 1)

            def transpose_wf(c, p):
                pe.wait_ge(wf_in[p], (c - p) * 16 + 32)
                at_least(pe, wfT_ready, c - 1)
                nc.tensor.transpose(ps[:, TAB[p], 0:P], wf_a[:, p, :], ident[:, :])
                nc.tensor.transpose(ps[:, TAB[p], P:E], wf_b[:, p, :], ident[0:EB, 0:EB]).then_inc(wfT_done, 1)

            for b in range(2):
                total(b)
                transpose_wf(b, b)
            with pe.Fori(1, NG // 2) as i:
                for p in range(2):
                    total(2 * i + p)
                    transpose_wf(2 * i + p, p)
            with pe.Fori(NG, BITS) as b:
                total(b)

            pe.wait_ge(sel_step, 5)
            pe.wait_ge(kept_ready, BITS)
            nc.tensor.matmul(ps[:, CROSS, 0:1], pair[:, :], lt_count[:, :], start=True, stop=True).then_inc(cross_done, 1)
            nc.tensor.matmul(ps[:, CROSS, 1:2], lower[:, :], eq_count[:, :], start=True, stop=True).then_inc(cross_done, 1)
            pe.wait_ge(sel_step, 9)
            nc.tensor.matmul(ps[:, CROSS, 2:3], lower[:, :], chosen_count[:, :], start=True,
                             stop=True).then_inc(cross_done, 1)
            pe.wait_ge(sel_step, 12)
            for c in range(NCH):
                last = nc.tensor.transpose(ps[:, c // 4, (c % 4) * P:(c % 4 + 1) * P], row[5][:, c * P:(c + 1) * P],
                                           ident[:, :])
            last.then_inc(slotT_done, 1)

            pe.wait_ge(lohi_ready, 1)
            pe.wait_ge(wfT_ready, NG)

            def up(m):
                pe.wait_ge(fnT_ready, m + 1)
                pe.wait_ge(wT_vec, 2 * m + 2)
                pe.wait_ge(wT_act, m + 1)
                for s in range(3):
                    at_least(pe, hid_ready, 3 * m + s - 1)
                    for k in range(2):
                        o = ps[:, UP[s % 2], k * N:(k + 1) * N]
                        cols = slice((2 * s + k) * P, (2 * s + k + 1) * P)
                        nc.tensor.matmul(o, wT_a[:, cols], hnT_a[:, :], start=True, stop=False)
                        last = nc.tensor.matmul(o, wT_b[:, cols], hnT_b[:, :], start=False, stop=True)
                    last.then_inc(up_done, 1)

            def transposes(m, g):
                pe.wait_ge(fn_ready, m + 1)
                at_least(pe, fnT_ready, m)
                transpose_tokens(FNT, hn2).then_inc(fnT_done, 1)
                if isinstance(m, int):
                    pe.wait_ge(rows_in[g], 16 * SLOTS * (m // UN + 1))
                else:
                    pe.wait_ge(rows_in[g], (m - g) * (16 * SLOTS // UN) + 16 * SLOTS)
                for s in range(3):
                    if s == 0:
                        at_least(pe, wT_vec, 2 * m)
                    elif s == 1:
                        at_least(pe, wT_act, m)
                    else:
                        pe.wait_ge(wT_vec, 2 * m + 1)
                    for k in range(2):
                        rows = gathered[g][:, 2 * s + k, :]
                        nc.tensor.transpose(ps[:, WT[s % 2], k * P:(k + 1) * P], rows[:, 0:P], ident[:, :])
                        last = nc.tensor.transpose(ps[0:EB, WT[s % 2], (2 + k) * P:(3 + k) * P], rows[:, P:E],
                                                   ident[:, :])
                    last.then_inc(wT_done, 1)

            def make_list(m):
                pe.wait_ge(hi_vals_ready, m + 1)
                pe.wait_ge(onehot_ready, 2 * m + 2)
                at_least(pe, index_ready, m)
                for g in range(NG):
                    last = nc.tensor.matmul(ps[0:LO, LIST, 0:2 * HI], onehot_lo[:, g, :],
                                            hi_vals[:, g, :, :].rearrange("p a h -> p (a h)"),
                                            start=(g == 0), stop=(g == NG - 1))
                last.then_inc(list_done, 1)

            def down(m, g):
                pe.wait_ge(hid_ready, 3 * m + 3)
                at_least(pe, final_ready, m - 1)
                for h in range(2):
                    for s in range(SLOTS):
                        last = nc.tensor.matmul(ps[0:HALF, DOWN[g % 2], h * E:(h + 1) * E],
                                                hidden[:, s, h * HALF:(h + 1) * HALF], gathered[g][:, s, E:2 * E],
                                                start=(s == 0), stop=(s == SLOTS - 1))
                last.then_inc(down_done, 1)

            def step2(n, q, on):
                if on(3):
                    up(n - 3)
                if on(2):
                    transposes(n - 2, (q - 2) % UN)
                if on(0):
                    make_list(n)
                if on(3):
                    down(n - 3, (q - 3) % UN)

            over_images(pe, UN, LAG2, step2)


_INS = ['x', 'L0_tok_w_proj', 'L0_tok_b_proj', 'L0_tok_ln_gamma', 'L0_tok_ln_beta', 'L0_attn_w_qkv',
        'L0_attn_w_proj', 'L0_attn_b_proj', 'L0_ffn_w1', 'L0_ffn_w2', 'L0_ffn_w_mfc', 'L0_ffn_w_proj']
_OUT = ((64, 196, 192), 'float32')


def kernel(**inputs):
    import numpy as _np
    import concourse.bacc as _bacc
    from concourse import mybir as _mybir
    from concourse.bass_utils import run_bass_kernel_spmd as _run

    nc = _bacc.Bacc("TRN2", target_bir_lowering=False, num_devices=1)
    arrays, args = {}, []
    for name in _INS:
        a = _np.ascontiguousarray(inputs[name])
        arrays[f"in_{name}_dram"] = a
        args.append(nc.dram_tensor(f"in_{name}_dram", a.shape, _mybir.dt.from_np(a.dtype), kind="ExternalInput").ap())
    shape, dtype = _OUT
    args.append(nc.dram_tensor("out_dram", shape, _mybir.dt.from_np(_np.dtype(dtype)), kind="ExternalOutput").ap())
    vit_tower(nc, *args)
    r = _run(nc, [arrays], core_ids=[0])
    return r.results[0]["out_dram"]
```

```python
from contextlib import ExitStack

import concourse.bass as bass
from concourse import mybir

F32 = mybir.dt.float32
F16 = mybir.dt.float16
BF16 = mybir.dt.bfloat16
I32 = mybir.dt.int32
U32 = mybir.dt.uint32
ALU = mybir.AluOpType
ACT = mybir.ActivationFunctionType
AX_X = mybir.AxisListType.X

P = 128
EPS = 1e-5
EXP_UNDERFLOW = 87.336544
S_TOK = 16.0
S_HN = 4.0
S_QKV = 64.0
S_MFC = 16.0
S_FFN = 64.0
S_OUT = S_HN * S_MFC * S_FFN


def vit_tower(nc, x, w_tok, b_tok, gamma, beta, w_qkv, w_attn, b_attn, w1, w2, w_mfc, w_ffn, out):
    B, C_IN, IMG, _ = x.shape
    PATCH = 16
    G = IMG // PATCH
    N = G * G
    HALF = N // 2
    E = w_tok.shape[1]
    EB = E - P
    F = w_mfc.shape[0]
    R = w1.shape[0]
    K = 4 * E
    ROWS = C_IN * PATCH
    ODD = 64
    KX = ODD + ROWS
    JH = PATCH // 2
    SLOTS = K // P
    FH = F // 2
    NCH = FH // P
    NG = 2 * NCH
    ROW = 4 * E
    CHUNK = 2 * F // B
    LO = 32
    HI = K // LO
    UN = 4
    BANK = 512
    assert N % 2 == 0 and K % (P * LO // 32) == 0 and B % UN == 0 and 2 * B == P and HALF <= P

    table = nc.dram_tensor("ffn_table", (F, ROW), F16, kind="Internal").ap()
    tok_rows = w_tok.rearrange("(r j) e -> r j e", j=PATCH)
    out_rows = out.rearrange("b (h t) e -> b t h e", h=2)

    ctx = ExitStack()
    with ctx:
        def sb(name, shape, dt=F32):
            return ctx.enter_context(nc.sbuf_tensor(name, shape, dt))

        def sem(name):
            return ctx.enter_context(nc.semaphore(name))

        resid = sb("resid", [P, 2 * B, E])
        arena = sb("arena", [P, UN * SLOTS * 2 * E])
        patches = [arena[:, p * N * PATCH:(p + 1) * N * PATCH].rearrange("p (t j) -> p t j", j=PATCH)
                   for p in range(2)]
        row = [arena[:, s * FH:(s + 1) * FH] for s in range(6)]
        w2T = arena[0:R, 4 * FH:6 * FH]
        gathered = [arena[:, g * SLOTS * 2 * E:(g + 1) * SLOTS * 2 * E].bitcast(F16)
                    .rearrange("p (s e) -> p s e", s=SLOTS) for g in range(UN)]
        lo_T = sb("lo_T", [P, NG, B], I32)
        hi_T = sb("hi_T", [P, NG, B], I32)
        wtok_in = lo_T[:, :, :].rearrange("p g b -> p (g b)").bitcast(F32).rearrange("p (j e) -> p j e", j=JH)
        wq_in_a = hi_T[:, :, :].rearrange("p g b -> p (g b)").bitcast(F32)[:, 0:3 * E]
        wq_in_b = hi_T[:, :, :].rearrange("p g b -> p (g b)").bitcast(F32)[0:EB, 3 * E:6 * E] \
            if 6 * E <= NG * B else None
        wtok_h = sb("wtok_h", [P, JH, E], F16)
        wtok_l = sb("wtok_l", [P, JH, E], F16)
        wq_ah = sb("wq_ah", [P, 3 * E], F16)
        wq_al = sb("wq_al", [P, 3 * E], F16)
        wq_b = sb("wq_b", [P, 3 * E], F16)
        work = sb("work", [P, 4 * N * JH], F16)
        x_h, x_l = (work[:, k * 2 * N * JH:(k + 1) * 2 * N * JH].rearrange("p (u t j) -> p u t j", u=2, j=JH)
                    for k in range(2))
        wp_a = sb("wp_a", [P, E])
        wp_b = sb("wp_b", [EB + 1, E])
        gam = sb("gam", [P, 2, E])
        bet = sb("bet", [P, 2, E])
        ident = sb("ident", [P, P])
        ident16 = sb("ident16", [P, P], F16)
        pair = sb("pair", [P, P])
        swap = sb("swap", [P, P])
        lower = sb("lower", [P, P])
        mean_col = sb("mean_col", [P, 1])
        eps = sb("eps", [P, 3])
        stats = sb("stats", [P, 3, 2, 6])
        mv = sb("mv", [P, 3, 2, 2])
        sd = sb("sd", [P, 3, 2])
        rs = sb("rs", [P, 2, 2])
        z1 = sb("z1", [P, 2, E])
        z2 = sb("z2", [P, 2, E])
        hn = sb("hn", [P, 2, E])
        hn2 = sb("hn2", [P, 2, E])
        hnT_ah = sb("hnT_ah", [P, N], F16)
        hnT_al = sb("hnT_al", [P, N], F16)
        hnT_bh = sb("hnT_bh", [P, N], F16)
        hnT_bl = sb("hnT_bl", [EB, N], F16)
        ffn_mean = sb("ffn_mean", [P, 2 * B])
        ffn_rstd = sb("ffn_rstd", [P, 2 * B])
        q_s = sb("q_s", [P, 2, N])
        k2 = sb("k2", [P, 2, N])
        act_junk = sb("act_junk", [P, 4, N])
        vq = sb("vq", [P, 2, N])
        sums = sb("sums", [P, 2, 2])
        squares = sb("squares", [P, 2, 2])
        roots_in = sb("roots_in", [P, 2])
        roots = sb("roots", [P, 2, 2])
        sqsk = sb("sqsk", [P, 2])
        denom = sb("denom", [P, 2, 2])
        coef = sb("coef", [P, 2])
        yT_a = sb("yT_a", [P, 2, N])
        yT_b = sb("yT_b", [EB + 1, 2, N])
        pooled_a = sb("pooled_a", [P, B])
        pooled_b = sb("pooled_b", [EB, B])
        w1T_a = sb("w1T_a", [P, R])
        w1T_b = sb("w1T_b", [EB, R])
        w2_rows = sb("w2_rows", [P, NG, R])
        router = sb("router", [R, B])
        top = sb("top", [P, 1])
        top_both = sb("top_both", [P, 1])
        count = sb("count", [P, 1])
        lt_count = sb("lt_count", [P, 1])
        eq_count = sb("eq_count", [P, 1])
        ties_left = sb("ties_left", [P, 1])
        ties_before = sb("ties_before", [P, 1])
        chosen_count = sb("chosen_count", [P, 1])
        chosen_before = sb("chosen_before", [P, 1])
        bit = sb("bit", [P, 1], I32)
        bound = sb("bound", [P, 1], I32)
        trial = sb("trial", [P, 1], I32)
        kept_bit = sb("kept_bit", [P, 1], I32)
        iota32 = sb("iota32", [P, LO], I32)
        group_no = sb("group_no", [P, NG], BF16)
        feature_no = sb("feature_no", [P, 1])
        wm_in = sb("wm_in", [CHUNK, E])
        wf_a = sb("wf_a", [P, CHUNK])
        wf_b = sb("wf_b", [EB, CHUNK])
        tab_rows = sb("tab_rows", [CHUNK, ROW], F16)
        hi_vals = sb("hi_vals", [P, NG, 2, HI], BF16)
        groups_f = sb("groups_f", [LO, HI])
        index = [sb(f"index{p}", [P, SLOTS], U32) for p in range(2)]
        wT = work[:, 0:3 * K].rearrange("p (s a k f) -> p s a k f", s=3, a=3, k=2)
        at = 3 * K
        hid_h, hid_l = (work[:, at + k * SLOTS * N:at + (k + 1) * SLOTS * N].rearrange("p (s t) -> p s t", s=SLOTS)
                        for k in range(2))
        at += 2 * SLOTS * N
        onehot_lo = work[:, at:at + NG * LO].bitcast(BF16).rearrange("p (g v) -> p g v", g=NG)
        at += NG * LO
        onehot_hi = work[:, at:at + NG * HI].bitcast(BF16).rearrange("p (g v) -> p g v", g=NG)
        assert at + NG * HI <= 4 * N * JH
        final = sb("final", [P, 2, 2, E])
        ps = ctx.enter_context(nc.psum_tensor("ps", [P, 8, BANK], F32))
        EMB, TRN, QK_A, V_AB, QK_B, PRJ, TAB = (0, 1), 2, 3, 4, 5, 6, 7
        POOLED = 2 * E
        ROUTER, CROSS = 6, 7
        UP, WT, FNT, DOWN, LIST = (0, 1, 2), (3, 4), 5, 6, 7

        pads_set = sem("pads_set")
        fills_set = sem("fills_set")
        const_step = sem("const_step")
        consts_set = sem("consts_set")
        weights_in = sem("weights_in")
        x_in = [sem(f"x_in{p}") for p in range(2)]
        x_ready = sem("x_ready")
        embed_done = sem("embed_done")
        ln_stats = [sem(f"ln{k}_stats") for k in range(3)]
        ln_mv = [sem(f"ln{k}_mv") for k in range(3)]
        ln_sd = [sem(f"ln{k}_sd") for k in range(3)]
        ln_rs = [sem(f"ln{k}_rs") for k in range(3)]
        z1_ready = sem("z1_ready")
        z2_ready = sem("z2_ready")
        h1_ready = sem("h1_ready")
        hn_ready = sem("hn_ready")
        hnT_done = sem("hnT_done")
        hnT_ready = sem("hnT_ready")
        qkv_done = sem("qkv_done")
        sums_ready = sem("sums_ready")
        squares_ready = sem("squares_ready")
        roots_in_ready = sem("roots_in_ready")
        roots_ready = sem("roots_ready")
        sqsk_ready = sem("sqsk_ready")
        denom0_ready = sem("denom0_ready")
        denom_ready = sem("denom_ready")
        coef_ready = sem("coef_ready")
        vq_ready = sem("vq_ready")
        y_ready = sem("y_ready")
        proj_done = sem("proj_done")
        resid_ready = sem("resid_ready")
        hn2_ready = sem("hn2_ready")
        pool_done = sem("pool_done")
        pool_kept = sem("pool_kept")
        w2T_done = sem("w2T_done")
        w2T_ready = sem("w2T_ready")
        router_done = sem("router_done")
        router_ready = sem("router_ready")
        scores_done = sem("scores_done")
        sel_step = sem("sel_step")
        cross_done = sem("cross_done")
        trial_ready = sem("trial_ready")
        count_ready = sem("count_ready")
        total_done = sem("total_done")
        kept_ready = sem("kept_ready")
        bound_ready = sem("bound_ready")
        bit_ready = sem("bit_ready")
        wtok_h_ready = sem("wtok_h_ready")
        wtok_ready = sem("wtok_ready")
        wq_h_ready = sem("wq_h_ready")
        wq_ready = sem("wq_ready")
        x_h_ready = sem("x_h_ready")
        x_l_ready = sem("x_l_ready")
        hnT_h_ready = sem("hnT_h_ready")
        fnT_h_ready = sem("fnT_h_ready")
        hid_h_ready = sem("hid_h_ready")
        tab_in = sem("tab_in")
        tabT_done = sem("tabT_done")
        tab_h_ready = sem("tab_h_ready")
        tab_ready = sem("tab_ready")
        tab_out = sem("tab_out")
        slotT_done = sem("slotT_done")
        lohi_ready = sem("lohi_ready")
        onehot_ready = sem("onehot_ready")
        hi_vals_ready = sem("hi_vals_ready")
        list_done = sem("list_done")
        groups_f_ready = sem("groups_f_ready")
        index_ready = sem("index_ready")
        rows_in = [sem(f"rows_in{g}") for g in range(UN)]
        fn_ready = sem("fn_ready")
        fnT_done = sem("fnT_done")
        fnT_ready = sem("fnT_ready")
        wT_done = sem("wT_done")
        wT_ready = sem("wT_ready")
        up_done = sem("up_done")
        hid_ready = sem("hid_ready")
        down_done = sem("down_done")
        final_ready = sem("final_ready")
        vector_passed = sem("vector_passed")
        pool_passed = sem("pool_passed")
        stored = [sem(f"stored{p}") for p in range(2)]

        N_WEIGHTS = 17
        LAG1 = 6
        LAG2 = 4
        BITS = 31

        def over_images(eng, unroll, lag, body):
            first = max(2, lag // unroll + 1)
            for n in range(first * unroll):
                body(n, n % unroll, n // unroll, lambda k, n=n: 0 <= n - k < B)
            with eng.Fori(first, B // unroll) as i:
                for q in range(unroll):
                    body(unroll * i + q, q, i, lambda k: True)
            for n in range(B, B + lag):
                body(n, n % unroll, n // unroll, lambda k, n=n: 0 <= n - k < B)

        def at_least(eng, s, value):
            if not isinstance(value, int) or value > 0:
                eng.wait_ge(s, value)

        def image(m):
            return resid[0:HALF, bass.ds(2 * m, 2), :]

        block = ctx.enter_context(nc.Block())

        @block.sync
        def _(sp):
            gamma_row = gamma.rearrange("(a e) -> a e", a=1)
            beta_row = beta.rearrange("(a e) -> a e", a=1)
            loads = [
                (wtok_in[0:ROWS, :, :], tok_rows[:, 0:JH, :]),
                (wtok_in[ODD:KX, :, :], tok_rows[:, JH:PATCH, :]),
                (wtok_in[ROWS:ROWS + 1, 0, :], b_tok.rearrange("(a e) -> a e", a=1)),
            ]
            loads += [(t[0:HALF, h, :], r.to_broadcast([HALF, E]))
                      for t, r in ((gam, gamma_row), (bet, beta_row)) for h in range(2)]
            for rows, dst in ((slice(0, P), wq_in_a), (slice(P, E), wq_in_b)):
                three = w_qkv[rows, :].rearrange("c (m e) -> c m e", m=3)
                loads.append((dst[:, 0:3 * P].rearrange("c (m e) -> c m e", m=3), three[:, :, 0:P]))
                loads.append((dst[:, 3 * P:3 * E].rearrange("c (m e) -> c m e", m=3), three[:, :, P:E]))
            loads += [
                (wp_a[:, :], w_attn[0:P, :]),
                (wp_b[0:EB, :], w_attn[P:E, :]),
                (wp_b[EB:EB + 1, :], b_attn.rearrange("(a e) -> a e", a=1)),
                (w1T_a[:, :], w1.rearrange("r c -> c r")[0:P, :]),
                (w1T_b[:, :], w1.rearrange("r c -> c r")[P:E, :]),
                (w2_rows[:, :, :], w2.rearrange("(g p) r -> p g r", p=P)),
            ]
            assert len(loads) == N_WEIGHTS

            def load_x(n, p):
                at_least(sp, x_l_ready, n - 1)
                for c in range(C_IN):
                    src = x[bass.ds(n, 1), c, :, :].rearrange("b (g k) w -> k (b g) w", k=PATCH)
                    dst = patches[p][c * PATCH:(c + 1) * PATCH, :, :].rearrange("k (g t) j -> k g (t j)", g=G)
                    sp.dma_start(dst, src).then_inc(x_in[p], 16)

            sp.wait_ge(pads_set, 1)
            load_x(0, 0)
            for dst, src in loads[:3]:
                sp.dma_start(dst, src).then_inc(weights_in, 16)
            load_x(1, 1)
            with nc.allow_non_contiguous_dma(reason="w1 comes in transposed: 2304 words"):
                for dst, src in loads[3:]:
                    sp.dma_start(dst, src).then_inc(weights_in, 16)
            def load_tab(c):
                at_least(sp, tab_ready, c)
                feats = bass.ds(c * CHUNK, CHUNK)
                sp.dma_start(wm_in[:, :], w_mfc[feats, :]).then_inc(tab_in, 16)
                sp.dma_start(wf_a[:, :], w_ffn[0:P, feats]).then_inc(tab_in, 16)
                sp.dma_start(wf_b[:, :], w_ffn[P:E, feats]).then_inc(tab_in, 16)

            def store_tab(c):
                sp.wait_ge(tab_ready, c + 1)
                sp.dma_start(table[bass.ds(c * CHUNK, CHUNK), :], tab_rows[:, :]).then_inc(tab_out, 16)

            load_x(2, 0)
            load_tab(0)
            load_x(3, 1)
            with sp.Fori(2, B // 2) as i:
                load_x(2 * i, 0)
                store_tab(i - 2)
                load_tab(i - 1)
                load_x(2 * i + 1, 1)
            store_tab(B // 2 - 2)
            load_tab(B // 2 - 1)
            store_tab(B // 2 - 1)

            def store(m, p):
                sp.wait_ge(final_ready, m + 1)
                sp.dma_start(out_rows[bass.ds(m, 1), :, :, :].rearrange("b t h e -> (b t) h e"),
                             final[0:HALF, p, :, :]).then_inc(stored[p], 16)

            with sp.Fori(0, B // 2) as i:
                for p in range(2):
                    store(2 * i + p, p)
            for p in range(2):
                sp.wait_ge(stored[p], 16 * (B // 2))

        @block.gpsimd
        def _(pool):
            pool.iota(iota32[:, :], [[1, LO]], base=0, channel_multiplier=0)
            pool.iota(group_no[:, :], [[1, NCH], [NCH, 2]], base=0, channel_multiplier=0,
                      allow_small_or_imprecise_dtypes=True)
            pool.iota(feature_no[:, :], [[1, 1]], base=0, channel_multiplier=1,
                      allow_small_or_imprecise_dtypes=True)
            for m in (ident, ident16, pair, swap, lower):
                last = pool.memset(m[:, :], 0.0)
            last.then_inc(const_step, 1)
            turns = [(ident, 0), (ident16, 0), (pair, 0), (swap, B), (lower, B), (pair, B), (swap, -B), (pair, -B)]
            for k, (m, offset) in enumerate(turns):
                pool.wait_ge(const_step, k + 1)
                last = pool.affine_select(out=m[:, :], in_=m[:, :], compare_op=ALU.not_equal, fill=1.0,
                                          base=offset, pattern=[[-1, P]], channel_multiplier=1)
                last.then_inc(const_step if k + 1 < len(turns) else consts_set, 1)

            pool.wait_ge(weights_in, 16 * N_WEIGHTS)

            def affine(m):
                pool.wait_ge(z1_ready, m + 1)
                at_least(pool, h1_ready, m)
                pool.tensor_tensor(z2[0:HALF, :, :], z1[0:HALF, :, :], gam[0:HALF, :, :],
                                   ALU.mult).then_inc(z2_ready, 1)
                pool.wait_ge(z2_ready, m + 1)
                pool.tensor_tensor(image(m), z2[0:HALF, :, :], bet[0:HALF, :, :],
                                   ALU.add).then_inc(h1_ready, 1)

            def low_x(n, p):
                pool.wait_ge(x_h_ready, n + 1)
                at_least(pool, embed_done, n - 1)
                pool.tensor_tensor(x_l[0:KX, p, :, :], patches[p][0:KX, :, 0:JH], x_h[0:KX, p, :, :],
                                   ALU.subtract).then_inc(x_l_ready, 1)

            def step1(n, p, i, on):
                if on(0):
                    low_x(n, p)
                if on(2):
                    affine(n - 2)

            over_images(pool, 2, 2, step1)

            pool.wait_ge(tab_out, 16 * (B // 2))

            def gather(m, g):
                pool.wait_ge(index_ready, m + 1)
                at_least(pool, down_done, m - UN + 1)
                pool.sem_inc(pool_passed)
                for s in range(SLOTS):
                    pool.indirect_dma_start(
                        gathered[g][:, s, :], None, table,
                        bass.IndirectOffsetOnAxis(index[g % 2][:, s:s + 1], 0)).then_inc(rows_in[g], 16)

            def step(n, q, i, on):
                if on(1):
                    gather(n - 1, (q - 1) % UN)

            over_images(pool, UN, 1, step)

        @block.scalar
        def _(act):
            def sqrt_of_var(k, m):
                act.wait_ge(ln_mv[k], m + 1)
                at_least(act, ln_rs[k], m)
                nc.scalar.activation(sd[0:HALF, k, :], mv[0:HALF, k, :, 1], ACT.Sqrt,
                                     bias=eps[0:HALF, k:k + 1]).then_inc(ln_sd[k], 1)

            def join_x(n, p):
                act.wait_ge(x_in[p], 16 * C_IN * (n // 2 + 1) if isinstance(n, int) else (n - p) * (8 * C_IN) + 16 * C_IN)
                nc.scalar.activation(patches[p][ODD:KX, :, 0:JH], patches[p][0:ROWS, :, JH:PATCH],
                                     ACT.Copy).then_inc(x_ready, 1)

            def high_x(n, p):
                act.wait_ge(x_ready, n + 1)
                at_least(act, embed_done, n - 1)
                nc.scalar.activation(x_h[0:KX, p, :, :], patches[p][0:KX, :, 0:JH], ACT.Copy).then_inc(x_h_ready, 1)

            def high_tokens(bank, ready):
                for dst, rows in ((hnT_ah[:, :], slice(0, P)), (hnT_bh[0:EB, :], None), (hnT_bh[EB:P, :], None)):
                    src = ps[rows, bank, 0:N] if rows else ps[0:EB, bank, 256:256 + N]
                    last = nc.scalar.activation(dst, src, ACT.Copy, scale=S_HN)
                last.then_inc(ready, 1)

            def copy_hnT(m):
                act.wait_ge(hnT_done, m + 1)
                at_least(act, qkv_done, m)
                high_tokens(TRN, hnT_h_ready)

            def high_tab(c):
                act.wait_ge(tabT_done, c + 1)
                at_least(act, tab_out, 16 * c)
                nc.scalar.activation(tab_rows[:, 0:P], wm_in[:, 0:P], ACT.Copy, scale=S_MFC)
                nc.scalar.activation(tab_rows[:, 2 * P:2 * P + EB], wm_in[:, P:E], ACT.Copy, scale=S_MFC)
                nc.scalar.activation(tab_rows[:, 2 * E:3 * E], ps[0:CHUNK, TAB, 0:E], ACT.Copy,
                                     scale=S_FFN).then_inc(tab_h_ready, 1)

            def attention_sums(m):
                act.wait_ge(qkv_done, m + 1)
                at_least(act, y_ready, m)
                nc.scalar.activation(q_s[:, 0, :], ps[:, QK_A, 0:N], ACT.Identity, accum_out=sums[:, 0, 0:1])
                nc.scalar.activation(q_s[0:EB, 1, :], ps[0:EB, QK_B, 0:N], ACT.Identity,
                                     accum_out=sums[0:EB, 0, 1:2])
                nc.scalar.activation(act_junk[:, 0, :], ps[:, QK_A, N:2 * N], ACT.Identity,
                                     accum_out=sums[:, 1, 0:1])
                nc.scalar.activation(act_junk[0:EB, 3, :], ps[EB:2 * EB, QK_B, 0:N], ACT.Identity,
                                     accum_out=sums[0:EB, 1, 1:2]).then_inc(sums_ready, 1)
                nc.scalar.activation(act_junk[:, 1, :], ps[:, QK_A, 0:N], ACT.Square, accum_out=squares[:, 0, 0:1])
                nc.scalar.activation(act_junk[0:EB, 2, :], ps[0:EB, QK_B, 0:N], ACT.Square,
                                     accum_out=squares[0:EB, 0, 1:2])
                nc.scalar.activation(k2[:, 0, :], ps[:, QK_A, N:2 * N], ACT.Square, accum_out=squares[:, 1, 0:1])
                nc.scalar.activation(k2[0:EB, 1, :], ps[EB:2 * EB, QK_B, 0:N], ACT.Square,
                                     accum_out=squares[0:EB, 1, 1:2]).then_inc(squares_ready, 1)

            def attention_roots(m):
                act.wait_ge(roots_in_ready, m + 1)
                act.wait_ge(squares_ready, m + 1)
                nc.scalar.activation(roots[:, 0, :], roots_in[:, :], ACT.Sqrt)
                nc.scalar.activation(roots[:, 1, :], squares[:, 1, :], ACT.Sqrt,
                                     scale=(S_HN * S_QKV) ** 2).then_inc(roots_ready, 1)

            act.wait_ge(fills_set, 1)
            act.wait_ge(weights_in, 16 * N_WEIGHTS)
            nc.scalar.activation(wtok_h[0:KX, :, :], wtok_in[0:KX, :, :], ACT.Copy,
                                 scale=S_TOK).then_inc(wtok_h_ready, 1)
            nc.scalar.activation(wq_ah[:, :], wq_in_a, ACT.Copy, scale=S_QKV)
            nc.scalar.activation(wq_b[0:EB, :], wq_in_b, ACT.Copy, scale=S_QKV).then_inc(wq_h_ready, 1)

            def step1(n, p, i, on):
                if on(4):
                    sqrt_of_var(1, n - 4)
                if on(3):
                    sqrt_of_var(0, n - 3)
                if on(1):
                    high_x(n - 1, 1 - p)
                if on(5):
                    attention_sums(n - 5)
                if on(7):
                    sqrt_of_var(2, n - 7)
                if on(5):
                    attention_roots(n - 5)
                if on(4):
                    copy_hnT(n - 4)
                if on(0):
                    join_x(n, p)
                if p == 1 and on(3):
                    high_tab(i - 1)

            over_images(act, 2, LAG1 + 1, step1)

            act.wait_ge(w2T_done, 1)
            for c in range(F // BANK):
                last = nc.scalar.activation(w2T[:, c * BANK:(c + 1) * BANK], ps[0:R, c, :], ACT.Copy)
            last.then_inc(w2T_ready, 1)
            act.wait_ge(router_done, 1)
            nc.scalar.activation(router[:, :], ps[0:R, ROUTER, 0:B], ACT.Relu).then_inc(router_ready, 1)

            def copy_fnT(m):
                act.wait_ge(fnT_done, m + 1)
                at_least(act, up_done, 3 * m)
                high_tokens(FNT, fnT_h_ready)

            def copy_wT(m):
                at_least(act, up_done, 3 * m)
                for s in range(3):
                    act.wait_ge(wT_done, 3 * m + s + 1)
                    nc.scalar.activation(wT[:, s, :, :, :].rearrange("p a k f -> p (a k f)"),
                                         ps[:, WT[s % 2], :].bitcast(F16)[:, 0:6 * P], ACT.Copy).then_inc(wT_ready, 1)

            def relu(m):
                at_least(act, down_done, m)
                for s in range(3):
                    act.wait_ge(up_done, 3 * m + s + 1)
                    nc.scalar.activation(hid_h[:, 2 * s:2 * s + 2, :].rearrange("p s t -> p (s t)"),
                                         ps[:, UP[s], 0:2 * N], ACT.Relu).then_inc(hid_h_ready, 1)

            def step2(n, q, i, on):
                if on(4):
                    relu(n - 4)
                if on(3):
                    copy_fnT(n - 3)
                    copy_wT(n - 3)

            over_images(act, UN, LAG2, step2)

        @block.vector
        def _(dve):
            nc.vector.memset(patches[0][32:64, :, :], 1.0)
            nc.vector.memset(patches[1][32:64, :, :], 1.0)
            nc.vector.memset(wtok_in[32:64, :, :], 0.0).then_inc(pads_set, 1)
            nc.vector.memset(eps[:, 0:1], EPS * S_TOK * S_TOK)
            nc.vector.memset(eps[:, 1:3], EPS)
            nc.vector.memset(mean_col[:, :], 1.0 / N)
            nc.vector.memset(yT_b[EB:EB + 1, :, :], 1.0)
            nc.vector.memset(sums[:, :, :], 1.0)
            nc.vector.memset(squares[:, :, :], 1.0)
            nc.vector.memset(bit[:, :], 1 << (BITS - 1))
            nc.vector.memset(bound[:, :], 0).then_inc(fills_set, 1)

            def apart():
                dve.sem_inc(vector_passed)

            def collect(k, m, source, ready):
                dve.wait_ge(ready, m + 1)
                apart()
                for h in range(2):
                    last = nc.vector.bn_stats(stats[0:HALF, k, h, :], source(h))
                last.then_inc(ln_stats[k], 1)

            def aggregate(k, m):
                dve.wait_ge(ln_stats[k], m + 1)
                apart()
                for h in range(2):
                    last = nc.vector.bn_aggr(mv[0:HALF, k, h, :], stats[0:HALF, k, h, :])
                last.then_inc(ln_mv[k], 1)

            def invert(k, m):
                dve.wait_ge(ln_sd[k], m + 1)
                rstd = rs[0:HALF, k, :] if k < 2 else ffn_rstd[0:HALF, bass.ds(2 * m, 2)]
                nc.vector.reciprocal(rstd, sd[0:HALF, k, :]).then_inc(ln_rs[k], 1)

            def normalise(k, m, source, out_tile, out_ready, free):
                dve.wait_ge(ln_rs[k], m + 1)
                at_least(dve, free, m)
                for h in range(2):
                    r = rs[0:HALF, k, h:h + 1] if k < 2 else ffn_rstd[0:HALF, bass.ds(2 * m + h, 1)]
                    last = nc.vector.tensor_scalar(out_tile[0:HALF, h, :], source(h), mv[0:HALF, k, h, 0:1], r,
                                                   ALU.subtract, ALU.mult)
                last.then_inc(out_ready, 1)

            def embedded(p):
                return lambda h: ps[0:HALF, EMB[p], h * E:(h + 1) * E]

            def stream(m):
                return lambda h: image(m)[:, h, :]

            def attention_products(m):
                dve.wait_ge(sums_ready, m + 1)
                nc.vector.tensor_tensor(vq[:, 0, :], ps[:, V_AB, 0:N], q_s[:, 0, :], ALU.mult)
                nc.vector.tensor_tensor(vq[0:EB, 1, :], ps[0:EB, V_AB, N:2 * N], q_s[0:EB, 1, :],
                                        ALU.mult).then_inc(vq_ready, 1)
                nc.vector.tensor_tensor(sqsk[:, :], sums[:, 0, :], sums[:, 1, :], ALU.mult).then_inc(sqsk_ready, 1)

            def norm_products(m):
                dve.wait_ge(squares_ready, m + 1)
                nc.vector.tensor_tensor(roots_in[:, :], squares[:, 0, :], squares[:, 1, :],
                                        ALU.mult).then_inc(roots_in_ready, 1)

            def add_sums(m):
                dve.wait_ge(roots_ready, m + 1)
                dve.wait_ge(sqsk_ready, m + 1)
                nc.vector.scalar_tensor_tensor(out=denom[:, 0, :], in0=roots[:, 0, :], scalar=float(N),
                                               in1=sqsk[:, :], op0=ALU.mult,
                                               op1=ALU.add).then_inc(denom0_ready, 1)

            def multiply_by_k(m):
                dve.wait_ge(denom0_ready, m + 1)
                nc.vector.tensor_tensor(denom[:, 1, :], denom[:, 0, :], roots[:, 1, :],
                                        ALU.mult).then_inc(denom_ready, 1)

            def attention_result(m, p):
                dve.wait_ge(denom_ready, m + 1)
                nc.vector.reciprocal(coef[:, :], denom[:, 1, :]).then_inc(coef_ready, 1)
                dve.wait_ge(coef_ready, m + 1)
                dve.wait_ge(vq_ready, m + 1)
                at_least(dve, proj_done, m - 1)
                nc.vector.scalar_tensor_tensor(out=yT_a[:, p, :], in0=vq[:, 0, :], scalar=coef[:, 0:1],
                                               in1=k2[:, 0, :], op0=ALU.mult, op1=ALU.mult)
                nc.vector.scalar_tensor_tensor(out=yT_b[0:EB, p, :], in0=vq[0:EB, 1, :], scalar=coef[0:EB, 1:2],
                                               in1=k2[0:EB, 1, :], op0=ALU.mult,
                                               op1=ALU.mult).then_inc(y_ready, 1)

            def add_attention(m):
                dve.wait_ge(proj_done, m + 1)
                dve.wait_ge(hn_ready, m + 1)
                nc.vector.tensor_tensor(image(m), ps[0:HALF, PRJ, 0:2 * E].rearrange("p (h e) -> p h e", h=2),
                                        image(m), ALU.add).then_inc(resid_ready, 1)

            def keep_mean(m):
                nc.vector.tensor_copy(ffn_mean[0:HALF, bass.ds(2 * m, 2)], mv[0:HALF, 2, :, 0])

            def keep_pooled(m):
                dve.wait_ge(pool_done, m + 1)
                nc.vector.tensor_copy(pooled_a[:, bass.ds(m, 1)], ps[:, PRJ, POOLED:POOLED + 1])
                nc.vector.tensor_copy(pooled_b[:, bass.ds(m, 1)],
                                      ps[0:EB, PRJ, POOLED + 1:POOLED + 2]).then_inc(pool_kept, 1)

            dve.wait_ge(fills_set, 1)
            dve.wait_ge(wtok_h_ready, 1)
            nc.vector.scalar_tensor_tensor(out=wtok_l[0:KX, :, :], in0=wtok_in[0:KX, :, :], scalar=S_TOK,
                                           in1=wtok_h[0:KX, :, :], op0=ALU.mult,
                                           op1=ALU.subtract).then_inc(wtok_ready, 1)
            dve.wait_ge(wq_h_ready, 1)
            nc.vector.scalar_tensor_tensor(out=wq_al[:, :], in0=wq_in_a, scalar=S_QKV, in1=wq_ah[:, :],
                                           op0=ALU.mult, op1=ALU.subtract)
            nc.vector.scalar_tensor_tensor(out=wq_b[EB:P, :], in0=wq_in_b, scalar=S_QKV, in1=wq_b[0:EB, :],
                                           op0=ALU.mult, op1=ALU.subtract).then_inc(wq_ready, 1)

            def low_tokens(bank, ready):
                nc.vector.scalar_tensor_tensor(out=hnT_al[:, :], in0=ps[:, bank, 0:N], scalar=S_HN,
                                               in1=hnT_ah[:, :], op0=ALU.mult, op1=ALU.subtract)
                nc.vector.scalar_tensor_tensor(out=hnT_bl[:, :], in0=ps[0:EB, bank, 256:256 + N], scalar=S_HN,
                                               in1=hnT_bh[0:EB, :], op0=ALU.mult,
                                               op1=ALU.subtract).then_inc(ready, 1)

            def low_hnT(m):
                dve.wait_ge(hnT_h_ready, m + 1)
                at_least(dve, qkv_done, m)
                low_tokens(TRN, hnT_ready)

            def low_tab(c):
                dve.wait_ge(tab_h_ready, c + 1)
                for out_cols, src, high, scale in (
                    (slice(P, 2 * P), wm_in[:, 0:P], slice(0, P), S_MFC),
                    (slice(2 * P + EB, 2 * E), wm_in[:, P:E], slice(2 * P, 2 * P + EB), S_MFC),
                    (slice(3 * E, 4 * E), ps[0:CHUNK, TAB, 0:E], slice(2 * E, 3 * E), S_FFN),
                ):
                    last = nc.vector.scalar_tensor_tensor(out=tab_rows[:, out_cols], in0=src, scalar=scale,
                                                          in1=tab_rows[:, high], op0=ALU.mult, op1=ALU.subtract)
                last.then_inc(tab_ready, 1)


            def step1(n, p, i, on):
                if on(2):
                    collect(1, n - 2, stream(n - 2), h1_ready)
                if on(1):
                    collect(0, n - 1, embedded(1 - p), embed_done)
                if on(2):
                    aggregate(1, n - 2)
                if on(1):
                    aggregate(0, n - 1)
                if on(5):
                    add_attention(n - 5)
                if on(2):
                    invert(1, n - 2)
                if on(1):
                    invert(0, n - 1)
                if on(2):
                    normalise(1, n - 2, stream(n - 2), hn, hn_ready, hnT_done)
                if on(5):
                    collect(2, n - 5, stream(n - 5), resid_ready)
                if on(1):
                    normalise(0, n - 1, embedded(1 - p), z1, z1_ready, z2_ready)
                if on(5):
                    aggregate(2, n - 5)
                if p == 0 and on(2):
                    low_tab(i - 1)
                if on(6):
                    keep_pooled(n - 6)
                if on(3):
                    attention_products(n - 3)
                    norm_products(n - 3)
                if on(5):
                    invert(2, n - 5)
                    normalise(2, n - 5, stream(n - 5), hn2, hn2_ready, pool_done)
                if on(5):
                    keep_mean(n - 5)
                if on(3):
                    add_sums(n - 3)
                if on(3):
                    multiply_by_k(n - 3)
                    attention_result(n - 3, 1 - p)
                if on(2):
                    low_hnT(n - 2)

            over_images(dve, 2, LAG1, step1)

            done = 0

            def then(instruction):
                nonlocal done
                done += 1
                instruction.then_inc(sel_step, 1)
                dve.wait_ge(sel_step, done)

            scores = ps[:, 0:3, :].rearrange("p b c -> p (b c)")
            dist, below, tied, running, ones, slots = row[0], row[1], row[2], row[3], row[4], row[5]
            dve.wait_ge(scores_done, 1)
            nc.vector.memset(ones, 1.0)
            then(nc.vector.tensor_reduce(top[:, :], scores, AX_X, ALU.max))
            dve.wait_ge(cross_done, 1)
            then(nc.vector.tensor_tensor(top_both[:, :], ps[:, CROSS, 0:1], top[:, :], ALU.max))
            then(nc.vector.tensor_scalar(dist, scores, top_both[:, :], -1.0, ALU.subtract, ALU.mult))
            then(nc.vector.tensor_scalar(dist, dist, EXP_UNDERFLOW, None, ALU.min))

            def search_bit(b):
                at_least(dve, bound_ready, b)
                at_least(dve, bit_ready, b)
                nc.vector.tensor_tensor(trial[:, :], bound[:, :], bit[:, :], ALU.bitwise_or).then_inc(trial_ready, 1)
                dve.wait_ge(trial_ready, b + 1)
                nc.vector.tensor_scalar(below, dist, trial[:, :].bitcast(F32), 0.0, ALU.is_lt, ALU.add,
                                        accum_out=count[:, :]).then_inc(count_ready, 1)
                dve.wait_ge(total_done, b + 1)
                nc.vector.tensor_scalar(kept_bit[:, :], ps[:, CROSS, 0:1], K - 0.5, bit[:, :],
                                        ALU.is_lt, ALU.mult).then_inc(kept_ready, 1)
                dve.wait_ge(kept_ready, b + 1)
                nc.vector.tensor_tensor(bound[:, :], bound[:, :], kept_bit[:, :],
                                        ALU.bitwise_or).then_inc(bound_ready, 1)
                nc.vector.tensor_scalar(bit[:, :], bit[:, :], 1, None,
                                        ALU.logical_shift_right).then_inc(bit_ready, 1)

            search_bit(0)
            with dve.Fori(1, BITS) as b:
                search_bit(b)
            dve.wait_ge(bound_ready, BITS)

            kth = bound[:, :].bitcast(F32)
            nc.vector.tensor_scalar(below, dist, kth, 0.0, ALU.is_lt, ALU.add, accum_out=lt_count[:, :])
            then(nc.vector.tensor_scalar(tied, dist, kth, 0.0, ALU.is_equal, ALU.add, accum_out=eq_count[:, :]))
            dve.wait_ge(cross_done, 3)
            nc.vector.tensor_scalar(ties_left[:, :], ps[:, CROSS, 0:1], -1.0, float(K), ALU.mult, ALU.add)
            then(nc.vector.tensor_copy(ties_before[:, :], ps[:, CROSS, 1:2]))
            then(nc.vector.tensor_tensor_scan(running, ones, tied, ties_before[:, :], ALU.mult, ALU.add))
            then(nc.vector.scalar_tensor_tensor(out=tied, in0=running, scalar=ties_left[:, :], in1=tied,
                                                op0=ALU.is_le, op1=ALU.mult))
            then(nc.vector.scalar_tensor_tensor(out=below, in0=below, scalar=1.0, in1=tied, op0=ALU.mult,
                                                op1=ALU.add, accum_out=chosen_count[:, :]))
            dve.wait_ge(cross_done, 4)
            then(nc.vector.tensor_copy(chosen_before[:, :], ps[:, CROSS, 2:3]))
            then(nc.vector.tensor_tensor_scan(running, ones, below, chosen_before[:, :], ALU.mult, ALU.add))
            then(nc.vector.tensor_tensor(slots, running, below, ALU.mult))
            dve.wait_ge(slotT_done, 1)
            flat_hi = hi_T[:, :, :].rearrange("p g b -> p (g b)")
            flat_lo = lo_T[:, :, :].rearrange("p g b -> p (g b)")
            then(nc.vector.tensor_scalar(flat_hi, scores, -1.0, None, ALU.add))
            then(nc.vector.tensor_scalar(flat_lo, flat_hi, LO - 1, None, ALU.bitwise_and))
            nc.vector.tensor_scalar(flat_hi, flat_hi, LO.bit_length() - 1, None,
                                    ALU.arith_shift_right).then_inc(lohi_ready, 1)
            dve.wait_ge(lohi_ready, 1)

            def onehots(m):
                at_least(dve, list_done, m)
                at_least(dve, hi_vals_ready, m)
                values = iota32[:, :].unsqueeze(1)
                nc.vector.tensor_tensor(onehot_hi[:, :, :], hi_T[:, :, bass.ds(m, 1)].to_broadcast([P, NG, HI]),
                                        values[:, :, 0:HI].to_broadcast([P, NG, HI]),
                                        ALU.is_equal).then_inc(onehot_ready, 1)
                nc.vector.tensor_tensor(onehot_lo[:, :, :], lo_T[:, :, bass.ds(m, 1)].to_broadcast([P, NG, LO]),
                                        values.to_broadcast([P, NG, LO]), ALU.is_equal).then_inc(onehot_ready, 1)

            def list_values(m):
                dve.wait_ge(onehot_ready, 2 * m + 1)
                at_least(dve, list_done, m)
                nc.vector.tensor_tensor(hi_vals[:, :, 0, :], onehot_hi[:, :, :],
                                   group_no[:, :].unsqueeze(2).to_broadcast([P, NG, HI]), ALU.mult)
                nc.vector.tensor_scalar(hi_vals[:, :, 1, :], onehot_hi[:, :, :], feature_no[:, :], None,
                                   ALU.mult).then_inc(hi_vals_ready, 1)

            def write_index(m, q):
                dve.wait_ge(list_done, m + 1)
                at_least(dve, index_ready, m)
                nc.vector.tensor_scalar(groups_f[:, :], ps[0:LO, LIST, 0:HI], float(P), None,
                                        ALU.mult).then_inc(groups_f_ready, 1)
                dve.wait_ge(groups_f_ready, m + 1)
                g = (q - 2) % UN
                if isinstance(m, int):
                    at_least(dve, rows_in[g], 16 * SLOTS * ((m - 2) // UN + 1) if m >= 2 else 0)
                else:
                    dve.wait_ge(rows_in[g], (m - 2 - g) * (16 * SLOTS // UN) + 16 * SLOTS)
                for k in range(P // LO):
                    part = slice(k * SLOTS, (k + 1) * SLOTS)
                    last = nc.vector.tensor_tensor(index[q % 2][k * LO:(k + 1) * LO, :], groups_f[:, part],
                                                   ps[0:LO, LIST, HI + k * SLOTS:HI + (k + 1) * SLOTS], ALU.add)
                last.then_inc(index_ready, 1)

            def normalise_again(m):
                at_least(dve, fnT_done, m)
                for h in range(2):
                    last = nc.vector.tensor_scalar(hn2[0:HALF, h, :], image(m)[:, h, :],
                                                   ffn_mean[0:HALF, bass.ds(2 * m + h, 1)],
                                                   ffn_rstd[0:HALF, bass.ds(2 * m + h, 1)],
                                                   ALU.subtract, ALU.mult)
                last.then_inc(fn_ready, 1)

            def low_fnT(m):
                dve.wait_ge(fnT_h_ready, m + 1)
                at_least(dve, up_done, 3 * m)
                low_tokens(FNT, fnT_ready)

            def low_hidden(m):
                at_least(dve, down_done, m)
                for s in range(3):
                    dve.wait_ge(hid_h_ready, 3 * m + s + 1)
                    nc.vector.scalar_tensor_tensor(
                        out=hid_l[:, 2 * s:2 * s + 2, :].rearrange("p s t -> p (s t)"), in0=ps[:, UP[s], 0:2 * N],
                        scalar=0.0, in1=hid_h[:, 2 * s:2 * s + 2, :].rearrange("p s t -> p (s t)"),
                        op0=ALU.max, op1=ALU.subtract).then_inc(hid_ready, 1)

            def add_residual(m, q):
                dve.wait_ge(down_done, m + 1)
                if isinstance(m, int):
                    at_least(dve, stored[q % 2], 16 * (m // 2))
                else:
                    dve.wait_ge(stored[q % 2], (m - q % 2) * 8)
                nc.vector.scalar_tensor_tensor(
                    out=final[0:HALF, q % 2, :, :], in0=ps[0:HALF, DOWN, 0:2 * E].rearrange("p (h e) -> p h e", h=2),
                    scalar=1.0 / S_OUT, in1=image(m), op0=ALU.mult, op1=ALU.add).then_inc(final_ready, 1)

            def step2(n, q, i, on):
                if on(1):
                    write_index(n - 1, (q - 1) % UN)
                if on(4):
                    low_hidden(n - 4)
                if on(0):
                    onehots(n)
                    list_values(n)
                if on(3):
                    low_fnT(n - 3)
                if on(2):
                    normalise_again(n - 2)
                if on(4):
                    add_residual(n - 4, q)

            over_images(dve, UN, LAG2, step2)

        @block.tensor
        def _(pe):
            pe.wait_ge(consts_set, 1)
            pe.wait_ge(fills_set, 1)
            pe.wait_ge(weights_in, 16 * N_WEIGHTS)
            pe.wait_ge(wtok_ready, 1)
            pe.wait_ge(wq_ready, 1)

            def embed(n, p, h):
                if h == 0:
                    pe.wait_ge(x_h_ready, n + 1)
                    pe.wait_ge(x_l_ready, n + 1)
                    at_least(pe, z1_ready, n - 1)
                o = ps[0:HALF, EMB[p], h * E:(h + 1) * E]
                half = slice(h * HALF, (h + 1) * HALF)
                for j in range(JH):
                    nc.tensor.matmul(o, x_h[0:KX, p, half, j], wtok_h[0:KX, j, :], start=(j == 0), stop=False)
                    nc.tensor.matmul(o, x_h[0:KX, p, half, j], wtok_l[0:KX, j, :], start=False, stop=False)
                    last = nc.tensor.matmul(o, x_l[0:KX, p, half, j], wtok_h[0:KX, j, :], start=False,
                                            stop=(j == JH - 1))
                if h == 1:
                    last.then_inc(embed_done, 1)

            def transpose_tokens(bank, source):
                for h in range(2):
                    nc.tensor.transpose(ps[:, bank, h * HALF:(h + 1) * HALF], source[0:HALF, h, 0:P],
                                        ident[0:HALF, 0:HALF])
                    last = nc.tensor.transpose(ps[0:EB, bank, 256 + h * HALF:256 + (h + 1) * HALF],
                                               source[0:HALF, h, P:E], ident[0:HALF, 0:HALF])
                return last

            def channels_product(o, w_high, w_low, w_last):
                nc.tensor.matmul(o, w_high, hnT_ah[:, :], start=True, stop=False)
                nc.tensor.matmul(o, w_high, hnT_al[:, :], start=False, stop=False)
                nc.tensor.matmul(o, w_low, hnT_ah[:, :], start=False, stop=False)
                nc.tensor.matmul(o, w_last, hnT_bh[:, :], start=False, stop=False)
                return nc.tensor.matmul(o, w_last[0:EB], hnT_bl[:, :], start=False, stop=True)

            def transpose_normalised(m):
                pe.wait_ge(hn_ready, m + 1)
                at_least(pe, hnT_ready, m)
                transpose_tokens(TRN, hn).then_inc(hnT_done, 1)

            def qkv(m):
                pe.wait_ge(hnT_ready, m + 1)
                at_least(pe, vq_ready, m)
                at_least(pe, squares_ready, m)
                for out_ap, first, width in (
                    (ps[:, QK_A, 0:N], 0, P), (ps[:, QK_A, N:2 * N], P, P),
                    (ps[:, V_AB, 0:N], 2 * P, P), (ps[0:EB, V_AB, N:2 * N], 3 * P + 2 * EB, EB),
                    (ps[:, QK_B, 0:N], 3 * P, 2 * EB),
                ):
                    cols = slice(first, first + width)
                    last = channels_product(out_ap, wq_ah[:, cols], wq_al[:, cols], wq_b[:, cols])
                last.then_inc(qkv_done, 1)

            def project(m, p):
                pe.wait_ge(y_ready, m + 1)
                at_least(pe, resid_ready, m)
                at_least(pe, pool_kept, m - 1)
                for h in range(2):
                    o = ps[0:HALF, PRJ, h * E:(h + 1) * E]
                    half = slice(h * HALF, (h + 1) * HALF)
                    nc.tensor.matmul(o, yT_a[:, p, half], wp_a[:, :], start=True, stop=False)
                    last = nc.tensor.matmul(o, yT_b[:, p, half], wp_b[:, :], start=False, stop=True)
                last.then_inc(proj_done, 1)

            def pool_tokens(m):
                pe.wait_ge(hn2_ready, m + 1)
                pe.wait_ge(resid_ready, min(m + 2, B) if isinstance(m, int) else m + 2)
                for o, chans in ((ps[:, PRJ, POOLED:POOLED + 1], slice(0, P)),
                                 (ps[0:EB, PRJ, POOLED + 1:POOLED + 2], slice(P, E))):
                    for h in range(2):
                        last = nc.tensor.matmul(o, hn2[0:HALF, h, chans], mean_col[0:HALF, :],
                                                start=(h == 0), stop=(h == 1))
                last.then_inc(pool_done, 1)

            def transpose_tab(c):
                pe.wait_ge(tab_in, 48 * c + 48)
                at_least(pe, tab_ready, c)
                nc.tensor.transpose(ps[0:CHUNK, TAB, 0:P], wf_a[:, :], ident[:, :])
                nc.tensor.transpose(ps[0:CHUNK, TAB, P:E], wf_b[:, :],
                                    ident[0:EB, 0:EB]).then_inc(tabT_done, 1)

            def step1(n, p, i, on):
                if on(0):
                    embed(n, p, 0)
                if on(3):
                    qkv(n - 3)
                if on(2):
                    transpose_normalised(n - 2)
                if p == 1 and on(0):
                    transpose_tab(i)
                if on(6):
                    pool_tokens(n - 6)
                if on(0):
                    embed(n, p, 1)
                if on(4):
                    project(n - 4, p)

            over_images(pe, 2, LAG1, step1)

            pe.wait_ge(pool_kept, B)
            pe.wait_ge(resid_ready, B)
            pe.wait_ge(y_ready, B)
            for g in range(NG):
                last = nc.tensor.transpose(ps[0:R, g // 4, (g % 4) * P:(g % 4 + 1) * P], w2_rows[:, g, :],
                                           ident[:, :])
            last.then_inc(w2T_done, 1)
            nc.tensor.matmul(ps[0:R, ROUTER, 0:B], w1T_a[:, :], pooled_a[:, :], start=True, stop=False)
            nc.tensor.matmul(ps[0:R, ROUTER, 0:B], w1T_b[:, :], pooled_b[:, :], start=False,
                             stop=True).then_inc(router_done, 1)
            pe.wait_ge(w2T_ready, 1)
            pe.wait_ge(router_ready, 1)
            for h in range(2):
                for c in range(FH // BANK):
                    first = h * FH + c * BANK
                    last = nc.tensor.matmul(ps[h * B:(h + 1) * B, c, :], router[:, :],
                                            w2T[:, first:first + BANK], start=True, stop=True)
            last.then_inc(scores_done, 1)
            pe.wait_ge(sel_step, 1)
            nc.tensor.matmul(ps[:, CROSS, 0:1], swap[:, :], top[:, :], start=True, stop=True).then_inc(cross_done, 1)
            pe.wait_ge(sel_step, 2)

            def total(b):
                pe.wait_ge(count_ready, b + 1)
                at_least(pe, kept_ready, b)
                nc.tensor.matmul(ps[:, CROSS, 0:1], pair[:, :], count[:, :], start=True,
                                 stop=True).then_inc(total_done, 1)

            total(0)
            with pe.Fori(1, BITS) as b:
                total(b)

            pe.wait_ge(sel_step, 5)
            pe.wait_ge(kept_ready, BITS)
            nc.tensor.matmul(ps[:, CROSS, 0:1], pair[:, :], lt_count[:, :], start=True, stop=True).then_inc(cross_done, 1)
            nc.tensor.matmul(ps[:, CROSS, 1:2], lower[:, :], eq_count[:, :], start=True, stop=True).then_inc(cross_done, 1)
            pe.wait_ge(sel_step, 9)
            nc.tensor.matmul(ps[:, CROSS, 2:3], lower[:, :], chosen_count[:, :], start=True,
                             stop=True).then_inc(cross_done, 1)
            pe.wait_ge(sel_step, 12)
            for c in range(NCH):
                last = nc.tensor.transpose(ps[:, c // 4, (c % 4) * P:(c % 4 + 1) * P], row[5][:, c * P:(c + 1) * P],
                                           ident[:, :])
            last.then_inc(slotT_done, 1)

            pe.wait_ge(lohi_ready, 1)

            def up(m):
                pe.wait_ge(fnT_ready, m + 1)
                pe.wait_ge(wT_ready, 3 * m + 3)
                at_least(pe, hid_ready, 3 * m)
                for s in range(3):
                    for k in range(2):
                        last = channels_product(ps[:, UP[s], k * N:(k + 1) * N], wT[:, s, 0, k, :],
                                                wT[:, s, 1, k, :], wT[:, s, 2, k, :])
                    last.then_inc(up_done, 1)

            def transpose_renormalised(m):
                pe.wait_ge(fn_ready, m + 1)
                at_least(pe, fnT_ready, m)
                transpose_tokens(FNT, hn2).then_inc(fnT_done, 1)

            def transpose_rows(m, g, groups):
                if isinstance(m, int):
                    pe.wait_ge(rows_in[g], 16 * SLOTS * (m // UN + 1))
                else:
                    pe.wait_ge(rows_in[g], (m - g) * (16 * SLOTS // UN) + 16 * SLOTS)
                for s in groups:
                    at_least(pe, wT_ready, 3 * m + s - 1)
                    for k in range(2):
                        for a in range(3):
                            first = (2 * a + k) * P
                            last = nc.tensor.transpose(ps[:, WT[s % 2], :].bitcast(F16)[:, first:first + P],
                                                       gathered[g][:, 2 * s + k, a * P:(a + 1) * P], ident16[:, :])
                    last.then_inc(wT_done, 1)

            def make_list(m):
                pe.wait_ge(hi_vals_ready, m + 1)
                pe.wait_ge(onehot_ready, 2 * m + 2)
                at_least(pe, index_ready, m)
                for g in range(NG):
                    last = nc.tensor.matmul(ps[0:LO, LIST, 0:2 * HI], onehot_lo[:, g, :],
                                            hi_vals[:, g, :, :].rearrange("p a h -> p (a h)"),
                                            start=(g == 0), stop=(g == NG - 1))
                last.then_inc(list_done, 1)

            def down(m, g):
                pe.wait_ge(hid_ready, 3 * m + 3)
                at_least(pe, final_ready, m)
                for h in range(2):
                    o = ps[0:HALF, DOWN, h * E:(h + 1) * E]
                    half = slice(h * HALF, (h + 1) * HALF)
                    for s in range(SLOTS):
                        w_high, w_low = gathered[g][:, s, 2 * E:3 * E], gathered[g][:, s, 3 * E:4 * E]
                        nc.tensor.matmul(o, hid_h[:, s, half], w_high, start=(s == 0), stop=False)
                        nc.tensor.matmul(o, hid_h[:, s, half], w_low, start=False, stop=False)
                        last = nc.tensor.matmul(o, hid_l[:, s, half], w_high, start=False, stop=(s == SLOTS - 1))
                last.then_inc(down_done, 1)

            def step2(n, q, i, on):
                if on(1):
                    make_list(n - 1)
                if on(4):
                    up(n - 4)
                if on(3):
                    transpose_renormalised(n - 3)
                    transpose_rows(n - 3, (q - 3) % UN, (0, 1))
                if on(4):
                    down(n - 4, q)
                if on(3):
                    transpose_rows(n - 3, (q - 3) % UN, (2,))

            over_images(pe, UN, LAG2, step2)


_INS = ['x', 'L0_tok_w_proj', 'L0_tok_b_proj', 'L0_tok_ln_gamma', 'L0_tok_ln_beta', 'L0_attn_w_qkv',
        'L0_attn_w_proj', 'L0_attn_b_proj', 'L0_ffn_w1', 'L0_ffn_w2', 'L0_ffn_w_mfc', 'L0_ffn_w_proj']
_OUT = ((64, 196, 192), 'float32')


def kernel(**inputs):
    import numpy as _np
    import concourse.bacc as _bacc
    from concourse import mybir as _mybir
    from concourse.bass_utils import run_bass_kernel_spmd as _run

    nc = _bacc.Bacc("TRN2", target_bir_lowering=False, num_devices=1)
    arrays, args = {}, []
    for name in _INS:
        a = _np.ascontiguousarray(inputs[name])
        arrays[f"in_{name}_dram"] = a
        args.append(nc.dram_tensor(f"in_{name}_dram", a.shape, _mybir.dt.from_np(a.dtype), kind="ExternalInput").ap())
    shape, dtype = _OUT
    args.append(nc.dram_tensor("out_dram", shape, _mybir.dt.from_np(_np.dtype(dtype)), kind="ExternalOutput").ap())
    vit_tower(nc, *args)
    r = _run(nc, [arrays], core_ids=[0])
    return r.results[0]["out_dram"]
```

```python
from contextlib import ExitStack

import concourse.bass as bass
from concourse import mybir

F32 = mybir.dt.float32
F16 = mybir.dt.float16
BF16 = mybir.dt.bfloat16
I32 = mybir.dt.int32
U32 = mybir.dt.uint32
U16 = mybir.dt.uint16
ALU = mybir.AluOpType
ACT = mybir.ActivationFunctionType
AX_X = mybir.AxisListType.X

P = 128
EPS = 1e-5
EXP_UNDERFLOW = 87.336544
S_TOK = 16.0
S_HN = 4.0
S_QKV = 64.0
S_MFC = 16.0
S_FFN = 64.0
S_OUT = S_HN * S_MFC * S_FFN


def vit_tower(nc, x, w_tok, b_tok, gamma, beta, w_qkv, w_attn, b_attn, w1, w2, w_mfc, w_ffn, out):
    B, C_IN, IMG, _ = x.shape
    PATCH = 16
    G = IMG // PATCH
    N = G * G
    HALF = N // 2
    E = w_tok.shape[1]
    EB = E - P
    F = w_mfc.shape[0]
    R = w1.shape[0]
    K = 4 * E
    ROWS = C_IN * PATCH
    ODD = 64
    KX = ODD + ROWS
    JH = PATCH // 2
    SLOTS = K // P
    FH = F // 2
    NCH = FH // P
    NG = 2 * NCH
    ROW = 4 * E
    CHUNK = 2 * F // B
    LO = 32
    HI = K // LO
    K_UP = LO * LO
    UN = 4
    BANK = 512
    TRIALS = 3
    ROUNDS = 8
    assert N % 2 == 0 and K % (P * LO // 32) == 0 and B % UN == 0 and 2 * B == P and HALF <= P

    table = nc.dram_tensor("ffn_table", (F, ROW), F16, kind="Internal").ap()
    tok_rows = w_tok.rearrange("(r j) e -> r j e", j=PATCH)
    out_rows = out.rearrange("b (h t) e -> b t h e", h=2)

    ctx = ExitStack()
    with ctx:
        def sb(name, shape, dt=F32):
            return ctx.enter_context(nc.sbuf_tensor(name, shape, dt))

        def sem(name):
            return ctx.enter_context(nc.semaphore(name))

        resid = sb("resid", [P, 2 * B, E])
        arena = sb("arena", [P, UN * SLOTS * 2 * E])
        patches = [arena[:, p * N * PATCH:(p + 1) * N * PATCH].rearrange("p (t j) -> p t j", j=PATCH)
                   for p in range(2)]
        row = [arena[:, s * FH:(s + 1) * FH] for s in range(6)]
        gathered = [arena[:, g * SLOTS * 2 * E:(g + 1) * SLOTS * 2 * E].bitcast(F16)
                    .rearrange("p (s e) -> p s e", s=SLOTS) for g in range(UN)]
        dist, below, tied, running, ones, slots = row
        dist_bits = dist.bitcast(U16).rearrange("p (f k) -> p f k", k=2)
        key, key_low = (running.bitcast(U16)[:, k * FH:(k + 1) * FH] for k in range(2))
        unread = [below.bitcast(U16)[:, t * FH:(t + 1) * FH] for t in range(2)]
        signs = tied.bitcast(F16)[:, 0:FH]
        lo_T = sb("lo_T", [P, NG, B], I32)
        hi_T = sb("hi_T", [P, NG, B], I32)
        flat_lo, flat_hi = (t[:, :, :].rearrange("p g b -> p (g b)") for t in (lo_T, hi_T))
        assert JH * E <= NG * B and 6 * E <= NG * B
        wtok_in = flat_lo.bitcast(F32)[:, 0:JH * E].rearrange("p (j e) -> p j e", j=JH)
        wq_in_a, wq_in_b = flat_hi.bitcast(F32)[:, 0:3 * E], flat_hi.bitcast(F32)[0:EB, 3 * E:6 * E]
        w2T = [t[0:R, :].bitcast(F32) for t in (flat_lo, flat_hi)]
        wtok_h = sb("wtok_h", [P, JH, E], F16)
        wtok_l = sb("wtok_l", [P, JH, E], F16)
        wq_ah = sb("wq_ah", [P, 3 * E], F16)
        wq_al = sb("wq_al", [P, 3 * E], F16)
        wq_b = sb("wq_b", [P, 3 * E], F16)
        work = sb("work", [P, 4 * N * JH], F16)
        x_h, x_l = (work[:, k * 2 * N * JH:(k + 1) * 2 * N * JH].rearrange("p (u t j) -> p u t j", u=2, j=JH)
                    for k in range(2))
        wp_a = sb("wp_a", [P, E])
        wp_b = sb("wp_b", [EB + 1, E])
        gam = sb("gam", [P, 2, E])
        bet = sb("bet", [P, 2, E])
        ident = sb("ident", [P, P])
        ident16 = sb("ident16", [P, P], F16)
        pair = sb("pair", [P, P])
        swap = sb("swap", [P, P])
        lower = sb("lower", [P, P])
        mean_col = sb("mean_col", [P, 1])
        eps = sb("eps", [P, 3])
        stats = sb("stats", [P, 3, 2, 6])
        mv = sb("mv", [P, 3, 2, 2])
        sd = sb("sd", [P, 3, 2])
        rs = sb("rs", [P, 2, 2])
        z1 = sb("z1", [P, 2, E])
        z2 = sb("z2", [P, 2, E])
        hn = sb("hn", [P, 2, E])
        hn2 = sb("hn2", [P, 2, E])
        hnT_ah = sb("hnT_ah", [P, N], F16)
        hnT_al = sb("hnT_al", [P, N], F16)
        hnT_bh = sb("hnT_bh", [P, N], F16)
        hnT_bl = sb("hnT_bl", [EB, N], F16)
        ffn_mean = sb("ffn_mean", [P, 2 * B])
        ffn_rstd = sb("ffn_rstd", [P, 2 * B])
        q_s = sb("q_s", [P, 2, N])
        k2 = sb("k2", [P, 2, N])
        act_unread = sb("act_unread", [P, 4, N])
        vq = sb("vq", [P, 2, N])
        sums = sb("sums", [P, 2, 2])
        squares = sb("squares", [P, 2, 2])
        roots_in = sb("roots_in", [P, 2])
        roots = sb("roots", [P, 2, 2])
        sqsk = sb("sqsk", [P, 2])
        denom = sb("denom", [P, 2, 2])
        coef = sb("coef", [P, 2])
        yT_a = sb("yT_a", [P, 2, N])
        yT_b = sb("yT_b", [EB + 1, 2, N])
        pooled_a = sb("pooled_a", [P, B])
        pooled_b = sb("pooled_b", [EB, B])
        w1T_a = sb("w1T_a", [P, R])
        w1T_b = sb("w1T_b", [EB, R])
        w2_rows = sb("w2_rows", [P, NG, R])
        router = sb("router", [R, B])
        tops = sb("tops", [P, FH // BANK])
        top = sb("top", [P, 1])
        top_both = sb("top_both", [P, 1])
        counts = sb("counts", [P, TRIALS])
        lt_count = sb("lt_count", [P, 1])
        eq_count = sb("eq_count", [P, 1])
        ties_left = sb("ties_left", [P, 1])
        chosen_count = sb("chosen_count", [P, 1])
        chosen_before = sb("chosen_before", [P, 1])
        offsets = sb("offsets", [P, ROUNDS + 1, TRIALS])
        step_size = sb("step_size", [P, ROUNDS])
        limits = sb("limits", [P, TRIALS])
        weights = sb("weights", [P, TRIALS])
        trials = sb("trials", [P, TRIALS])
        next_trials = sb("next_trials", [P, TRIALS])
        kept = sb("kept", [P, TRIALS])
        steps_up = sb("steps_up", [P, 1])
        bound = sb("bound", [P, 1])
        bound_high = sb("bound_high", [P, 1], I32)
        bound_low = sb("bound_low", [P, 1], I32)
        kth_bits = sb("kth_bits", [P, 1], I32)
        fewer = sb("fewer", [P, 1])
        exp_sum = sb("exp_sum", [P, 1])
        denominator = sb("denominator", [P, 1])
        log_sum = sb("log_sum", [P, 1])
        underflow = sb("underflow", [P, 1])
        iota32 = sb("iota32", [P, LO + HI], I32)
        group_no = sb("group_no", [P, NG], BF16)
        feature_no = sb("feature_no", [P, 1])
        wm_in = sb("wm_in", [CHUNK, E])
        wf_a = sb("wf_a", [P, CHUNK])
        wf_b = sb("wf_b", [EB, CHUNK])
        tab_rows = sb("tab_rows", [CHUNK, ROW], F16)
        hi_vals = sb("hi_vals", [P, NG, 2, HI], BF16)
        groups_f = sb("groups_f", [LO, HI])
        index = [sb(f"index{p}", [P, SLOTS], U32) for p in range(2)]
        wT = work[:, 0:3 * K].rearrange("p (s a k f) -> p s a k f", s=3, a=3, k=2)
        at = 3 * K
        hid_h, hid_l = (work[:, at + k * SLOTS * N:at + (k + 1) * SLOTS * N].rearrange("p (s t) -> p s t", s=SLOTS)
                        for k in range(2))
        at += 2 * SLOTS * N
        onehot_lo = work[:, at:at + NG * LO].bitcast(BF16).rearrange("p (g v) -> p g v", g=NG)
        at += NG * LO
        onehot_hi = work[:, at:at + NG * HI].bitcast(BF16).rearrange("p (g v) -> p g v", g=NG)
        assert at + NG * HI <= 4 * N * JH
        final = sb("final", [P, 2, 2, E])
        ps = ctx.enter_context(nc.psum_tensor("ps", [P, 8, BANK], F32))
        EMB, TRN, QK_A, V_AB, QK_B, PRJ, TAB = (0, 1), 2, 3, 4, 5, 6, 7
        POOLED = 2 * E
        ROUTER, CROSS = 6, 7
        UP, WT, FNT, DOWN, LIST = (0, 1, 2), (3, 4), 5, 6, 7

        pads_set = sem("pads_set")
        fills_set = sem("fills_set")
        const_step = sem("const_step")
        consts_set = sem("consts_set")
        wtok_landed = sem("wtok_landed")
        wq_landed = sem("wq_landed")
        weights_in = sem("weights_in")
        x_in = [sem(f"x_in{p}") for p in range(2)]
        x_ready = sem("x_ready")
        embed_done = sem("embed_done")
        ln_stats = [sem(f"ln{k}_stats") for k in range(3)]
        ln_mv = [sem(f"ln{k}_mv") for k in range(3)]
        ln_sd = [sem(f"ln{k}_sd") for k in range(3)]
        ln_rs = [sem(f"ln{k}_rs") for k in range(3)]
        z1_ready = sem("z1_ready")
        z2_ready = sem("z2_ready")
        h1_ready = sem("h1_ready")
        hn_ready = sem("hn_ready")
        hnT_done = sem("hnT_done")
        hnT_ready = sem("hnT_ready")
        qkv_done = sem("qkv_done")
        sums_ready = sem("sums_ready")
        squares_ready = sem("squares_ready")
        roots_in_ready = sem("roots_in_ready")
        roots_ready = sem("roots_ready")
        sqsk_ready = sem("sqsk_ready")
        denom0_ready = sem("denom0_ready")
        denom_ready = sem("denom_ready")
        coef_ready = sem("coef_ready")
        vq_ready = sem("vq_ready")
        y_ready = sem("y_ready")
        proj_done = sem("proj_done")
        resid_ready = sem("resid_ready")
        hn2_ready = sem("hn2_ready")
        pool_done = sem("pool_done")
        pool_kept = sem("pool_kept")
        w2T_done = sem("w2T_done")
        w2T_ready = sem("w2T_ready")
        router_done = sem("router_done")
        router_ready = sem("router_ready")
        scores_done = sem("scores_done")
        sel_step = sem("sel_step")
        ones_set = sem("ones_set")
        top_ready = sem("top_ready")
        top_both_ready = sem("top_both_ready")
        dist_ready = sem("dist_ready")
        low_key_ready = sem("low_key_ready")
        fewer_ready = sem("fewer_ready")
        exp_sum_ready = sem("exp_sum_ready")
        denominator_ready = sem("denominator_ready")
        log_sum_ready = sem("log_sum_ready")
        tie_counts_ready = sem("tie_counts_ready")
        chosen_ready = sem("chosen_ready")
        slots_ready = sem("slots_ready")
        cross_done = sem("cross_done")
        trial_ready = sem("trial_ready")
        count_ready = sem("count_ready")
        count_act = sem("count_act")
        total_done = sem("total_done")
        kept_ready = sem("kept_ready")
        bound_ready = sem("bound_ready")
        next_ready = sem("next_ready")
        wtok_h_ready = sem("wtok_h_ready")
        wtok_ready = sem("wtok_ready")
        wq_h_ready = sem("wq_h_ready")
        wq_ready = sem("wq_ready")
        x_h_ready = sem("x_h_ready")
        x_l_ready = sem("x_l_ready")
        hnT_h_ready = sem("hnT_h_ready")
        fnT_h_ready = sem("fnT_h_ready")
        hid_h_ready = sem("hid_h_ready")
        tab_in = sem("tab_in")
        tabT_done = sem("tabT_done")
        tab_h_ready = sem("tab_h_ready")
        tab_ready = sem("tab_ready")
        tab_out = sem("tab_out")
        slotT_done = sem("slotT_done")
        slot_copied = sem("slot_copied")
        lohi_ready = sem("lohi_ready")
        onehot_ready = sem("onehot_ready")
        hi_vals_ready = sem("hi_vals_ready")
        list_done = sem("list_done")
        groups_f_ready = sem("groups_f_ready")
        index_ready = sem("index_ready")
        rows_in = [sem(f"rows_in{g}") for g in range(UN)]
        fn_ready = sem("fn_ready")
        fnT_done = sem("fnT_done")
        fnT_ready = sem("fnT_ready")
        wT_done = sem("wT_done")
        wT_ready = sem("wT_ready")
        up_done = sem("up_done")
        hid_ready = sem("hid_ready")
        down_done = sem("down_done")
        final_ready = sem("final_ready")
        vector_passed = sem("vector_passed")
        pool_passed = sem("pool_passed")
        stored = [sem(f"stored{p}") for p in range(2)]

        N_WTOK, N_WQ, N_WEIGHTS = 3, 4, 10
        LAG1 = 6
        LAG2 = 4

        def over_images(eng, unroll, lag, body, after=None):
            first = max(2, lag // unroll + 1)
            for n in range(first * unroll):
                body(n, n % unroll, n // unroll, lambda k, n=n: 0 <= n - k < B)
                if after and n in after:
                    after[n]()
            with eng.Fori(first, B // unroll) as i:
                for q in range(unroll):
                    body(unroll * i + q, q, i, lambda k: True)
            for n in range(B, B + lag):
                body(n, n % unroll, n // unroll, lambda k, n=n: 0 <= n - k < B)

        def at_least(eng, s, value):
            if not isinstance(value, int) or value > 0:
                eng.wait_ge(s, value)

        def image(m):
            return resid[0:HALF, bass.ds(2 * m, 2), :]

        block = ctx.enter_context(nc.Block())

        @block.sync
        def _(sp):
            gamma_row = gamma.rearrange("(a e) -> a e", a=1)
            beta_row = beta.rearrange("(a e) -> a e", a=1)
            loads = [
                (wtok_in[0:ROWS, :, :], tok_rows[:, 0:JH, :]),
                (wtok_in[ODD:KX, :, :], tok_rows[:, JH:PATCH, :]),
                (wtok_in[ROWS:ROWS + 1, 0, :], b_tok.rearrange("(a e) -> a e", a=1)),
            ]
            loads += [(t[0:HALF, h, :], r.to_broadcast([HALF, E]))
                      for t, r in ((gam, gamma_row), (bet, beta_row)) for h in range(2)]
            wq_loads = []
            for rows, dst in ((slice(0, P), wq_in_a), (slice(P, E), wq_in_b)):
                three = w_qkv[rows, :].rearrange("c (m e) -> c m e", m=3)
                wq_loads.append((dst[:, 0:3 * P].rearrange("c (m e) -> c m e", m=3), three[:, :, 0:P]))
                wq_loads.append((dst[:, 3 * P:3 * E].rearrange("c (m e) -> c m e", m=3), three[:, :, P:E]))
            loads += [
                (wp_a[:, :], w_attn[0:P, :]),
                (wp_b[0:EB, :], w_attn[P:E, :]),
                (wp_b[EB:EB + 1, :], b_attn.rearrange("(a e) -> a e", a=1)),
                (w1T_a[:, :], w1.rearrange("r c -> c r")[0:P, :]),
                (w1T_b[:, :], w1.rearrange("r c -> c r")[P:E, :]),
                (w2_rows[:, :, :], w2.rearrange("(g p) r -> p g r", p=P)),
            ]
            assert len(loads) == N_WTOK + N_WEIGHTS and len(wq_loads) == N_WQ

            def load_x(n, p):
                at_least(sp, x_l_ready, n - 1)
                for c in range(C_IN):
                    src = x[bass.ds(n, 1), c, :, :].rearrange("b (g k) w -> k (b g) w", k=PATCH)
                    dst = patches[p][c * PATCH:(c + 1) * PATCH, :, :].rearrange("k (g t) j -> k g (t j)", g=G)
                    sp.dma_start(dst, src).then_inc(x_in[p], 16)

            sp.wait_ge(pads_set, 1)
            load_x(0, 0)
            sp.wait_ge(pads_set, 2)
            for dst, src in loads[:N_WTOK]:
                sp.dma_start(dst, src).then_inc(wtok_landed, 16)
            for dst, src in wq_loads:
                sp.dma_start(dst, src).then_inc(wq_landed, 16)
            sp.wait_ge(pads_set, 3)
            load_x(1, 1)
            with nc.allow_non_contiguous_dma(reason="w1 comes in transposed: 2304 words"):
                for dst, src in loads[N_WTOK:]:
                    sp.dma_start(dst, src).then_inc(weights_in, 16)
            def load_tab(c):
                at_least(sp, tab_ready, c)
                feats = bass.ds(c * CHUNK, CHUNK)
                sp.dma_start(wm_in[:, :], w_mfc[feats, :]).then_inc(tab_in, 16)
                sp.dma_start(wf_a[:, :], w_ffn[0:P, feats]).then_inc(tab_in, 16)
                sp.dma_start(wf_b[:, :], w_ffn[P:E, feats]).then_inc(tab_in, 16)

            def store_tab(c):
                sp.wait_ge(tab_ready, c + 1)
                sp.dma_start(table[bass.ds(c * CHUNK, CHUNK), :], tab_rows[:, :]).then_inc(tab_out, 16)

            load_x(2, 0)
            load_tab(0)
            load_x(3, 1)
            with sp.Fori(2, B // 2) as i:
                load_x(2 * i, 0)
                store_tab(i - 2)
                load_tab(i - 1)
                load_x(2 * i + 1, 1)
            store_tab(B // 2 - 2)
            load_tab(B // 2 - 1)
            store_tab(B // 2 - 1)

            def store(m, p):
                sp.wait_ge(final_ready, m + 1)
                sp.dma_start(out_rows[bass.ds(m, 1), :, :, :].rearrange("b t h e -> (b t) h e"),
                             final[0:HALF, p, :, :]).then_inc(stored[p], 16)

            with sp.Fori(0, B // 2) as i:
                for p in range(2):
                    store(2 * i + p, p)
            for p in range(2):
                sp.wait_ge(stored[p], 16 * (B // 2))

        @block.gpsimd
        def _(pool):
            pool.iota(iota32[:, :], [[1, LO + HI]], base=0, channel_multiplier=0)
            pool.iota(group_no[:, :], [[1, NCH], [NCH, 2]], base=0, channel_multiplier=0,
                      allow_small_or_imprecise_dtypes=True)
            pool.iota(feature_no[:, :], [[1, 1]], base=0, channel_multiplier=1,
                      allow_small_or_imprecise_dtypes=True)
            pool.memset(offsets[:, ROUNDS, :], 0.0)
            for r in range(ROUNDS):
                size = 4.0 ** (ROUNDS - 1 - r)
                pool.memset(step_size[:, r:r + 1], size)
                for t in range(TRIALS):
                    pool.memset(offsets[:, r, t:t + 1], (t + 1) * size - 0.5)
            for m in (ident, ident16, pair, swap, lower):
                last = pool.memset(m[:, :], 0.0)
            last.then_inc(const_step, 1)
            turns = [(ident, 0), (ident16, 0), (pair, 0), (swap, B), (lower, B), (pair, B), (swap, -B), (pair, -B)]
            for k, (m, offset) in enumerate(turns):
                pool.wait_ge(const_step, k + 1)
                last = pool.affine_select(out=m[:, :], in_=m[:, :], compare_op=ALU.not_equal, fill=1.0,
                                          base=offset, pattern=[[-1, P]], channel_multiplier=1)
                last.then_inc(const_step if k + 1 < len(turns) else consts_set, 1)

            def affine_weights():
                pool.wait_ge(weights_in, 16 * N_WEIGHTS)

            def affine(m):
                pool.wait_ge(z1_ready, m + 1)
                at_least(pool, h1_ready, m)
                pool.tensor_tensor(z2[0:HALF, :, :], z1[0:HALF, :, :], gam[0:HALF, :, :],
                                   ALU.mult).then_inc(z2_ready, 1)
                pool.wait_ge(z2_ready, m + 1)
                pool.tensor_tensor(image(m), z2[0:HALF, :, :], bet[0:HALF, :, :],
                                   ALU.add).then_inc(h1_ready, 1)

            def low_x(n, p):
                pool.wait_ge(x_h_ready, n + 1)
                at_least(pool, embed_done, n - 1)
                pool.tensor_tensor(x_l[0:KX, p, :, :], patches[p][0:KX, :, 0:JH], x_h[0:KX, p, :, :],
                                   ALU.subtract).then_inc(x_l_ready, 1)

            def step1(n, p, i, on):
                if on(0):
                    low_x(n, p)
                if on(2):
                    affine(n - 2)

            over_images(pool, 2, 2, step1, after={1: affine_weights})

            pool.memset(row[4], 1.0).then_inc(ones_set, 1)

            pool.wait_ge(tab_out, 16 * (B // 2))

            def gather(m, g):
                pool.wait_ge(index_ready, m + 1)
                at_least(pool, down_done, m - UN + 1)
                pool.sem_inc(pool_passed)
                for s in range(SLOTS):
                    pool.indirect_dma_start(
                        gathered[g][:, s, :], None, table,
                        bass.IndirectOffsetOnAxis(index[g % 2][:, s:s + 1], 0)).then_inc(rows_in[g], 16)

            def step(n, q, i, on):
                if on(1):
                    gather(n - 1, (q - 1) % UN)

            over_images(pool, UN, 1, step)

        @block.scalar
        def _(act):
            def sqrt_of_var(k, m):
                act.wait_ge(ln_mv[k], m + 1)
                at_least(act, ln_rs[k], m)
                nc.scalar.activation(sd[0:HALF, k, :], mv[0:HALF, k, :, 1], ACT.Sqrt,
                                     bias=eps[0:HALF, k:k + 1]).then_inc(ln_sd[k], 1)

            def join_x(n, p):
                if isinstance(n, int):
                    act.wait_ge(x_in[p], 16 * C_IN * (n // 2 + 1))
                else:
                    act.wait_ge(x_in[p], (n - p) * (8 * C_IN) + 16 * C_IN)
                nc.scalar.activation(patches[p][ODD:KX, :, 0:JH], patches[p][0:ROWS, :, JH:PATCH],
                                     ACT.Copy).then_inc(x_ready, 1)

            def high_x(n, p):
                act.wait_ge(x_ready, n + 1)
                at_least(act, embed_done, n - 1)
                nc.scalar.activation(x_h[0:KX, p, :, :], patches[p][0:KX, :, 0:JH], ACT.Copy).then_inc(x_h_ready, 1)

            def high_tokens(bank, ready):
                for dst, rows in ((hnT_ah[:, :], slice(0, P)), (hnT_bh[0:EB, :], None), (hnT_bh[EB:P, :], None)):
                    src = ps[rows, bank, 0:N] if rows else ps[0:EB, bank, 256:256 + N]
                    last = nc.scalar.activation(dst, src, ACT.Copy, scale=S_HN)
                last.then_inc(ready, 1)

            def copy_hnT(m):
                act.wait_ge(hnT_done, m + 1)
                at_least(act, qkv_done, m)
                high_tokens(TRN, hnT_h_ready)

            def high_tab(c):
                act.wait_ge(tabT_done, c + 1)
                at_least(act, tab_out, 16 * c)
                nc.scalar.activation(tab_rows[:, 0:P], wm_in[:, 0:P], ACT.Copy, scale=S_MFC)
                nc.scalar.activation(tab_rows[:, 2 * P:2 * P + EB], wm_in[:, P:E], ACT.Copy, scale=S_MFC)
                nc.scalar.activation(tab_rows[:, 2 * E:3 * E], ps[0:CHUNK, TAB, 0:E], ACT.Copy,
                                     scale=S_FFN).then_inc(tab_h_ready, 1)

            def attention_sums(m):
                act.wait_ge(qkv_done, m + 1)
                at_least(act, y_ready, m)
                nc.scalar.activation(q_s[:, 0, :], ps[:, QK_A, 0:N], ACT.Identity, accum_out=sums[:, 0, 0:1])
                nc.scalar.activation(q_s[0:EB, 1, :], ps[0:EB, QK_B, 0:N], ACT.Identity,
                                     accum_out=sums[0:EB, 0, 1:2])
                nc.scalar.activation(act_unread[:, 0, :], ps[:, QK_A, N:2 * N], ACT.Identity,
                                     accum_out=sums[:, 1, 0:1])
                nc.scalar.activation(act_unread[0:EB, 3, :], ps[EB:2 * EB, QK_B, 0:N], ACT.Identity,
                                     accum_out=sums[0:EB, 1, 1:2]).then_inc(sums_ready, 1)
                nc.scalar.activation(act_unread[:, 1, :], ps[:, QK_A, 0:N], ACT.Square, accum_out=squares[:, 0, 0:1])
                nc.scalar.activation(act_unread[0:EB, 2, :], ps[0:EB, QK_B, 0:N], ACT.Square,
                                     accum_out=squares[0:EB, 0, 1:2])
                nc.scalar.activation(k2[:, 0, :], ps[:, QK_A, N:2 * N], ACT.Square, accum_out=squares[:, 1, 0:1])
                nc.scalar.activation(k2[0:EB, 1, :], ps[EB:2 * EB, QK_B, 0:N], ACT.Square,
                                     accum_out=squares[0:EB, 1, 1:2]).then_inc(squares_ready, 1)

            def attention_roots(m):
                act.wait_ge(roots_in_ready, m + 1)
                act.wait_ge(squares_ready, m + 1)
                nc.scalar.activation(roots[:, 0, :], roots_in[:, :], ACT.Sqrt)
                nc.scalar.activation(roots[:, 1, :], squares[:, 1, :], ACT.Sqrt,
                                     scale=(S_HN * S_QKV) ** 2).then_inc(roots_ready, 1)

            def high_wq():
                act.wait_ge(fills_set, 1)
                act.wait_ge(wq_landed, 16 * N_WQ)
                nc.scalar.activation(wq_ah[:, :], wq_in_a, ACT.Copy, scale=S_QKV)
                nc.scalar.activation(wq_b[0:EB, :], wq_in_b, ACT.Copy, scale=S_QKV).then_inc(wq_h_ready, 1)

            def copy_w2T():
                act.wait_ge(w2T_done, 1)
                act.wait_ge(wtok_ready, 1)
                act.wait_ge(wq_ready, 1)
                for c in range(F // BANK):
                    h, first = divmod(c * BANK, FH)
                    last = nc.scalar.activation(w2T[h][:, first:first + BANK], ps[0:R, 2 + c, :], ACT.Copy)
                last.then_inc(w2T_ready, 1)

            act.wait_ge(wtok_landed, 16 * N_WTOK)
            nc.scalar.activation(wtok_h[0:KX, :, :], wtok_in[0:KX, :, :], ACT.Copy,
                                 scale=S_TOK).then_inc(wtok_h_ready, 1)

            def step1(n, p, i, on):
                if on(1):
                    high_x(n - 1, 1 - p)
                if on(4):
                    sqrt_of_var(1, n - 4)
                if on(3):
                    sqrt_of_var(0, n - 3)
                if on(5):
                    attention_sums(n - 5)
                if on(7):
                    sqrt_of_var(2, n - 7)
                if on(5):
                    attention_roots(n - 5)
                if on(4):
                    copy_hnT(n - 4)
                if on(0):
                    join_x(n, p)
                if p == 1 and on(3):
                    high_tab(i - 1)

            over_images(act, 2, LAG1 + 1, step1, after={1: high_wq, 2: copy_w2T})

            act.wait_ge(router_done, 1)
            nc.scalar.activation(router[:, :], ps[0:R, ROUTER, 0:B], ACT.Relu).then_inc(router_ready, 1)

            def count_third(r, starts):
                act.wait_ge(trial_ready, r + starts)
                nc.scalar.activation(signs, key, ACT.Sign, bias=trials[:, TRIALS - 1:TRIALS], scale=-1.0,
                                     accum_out=counts[:, TRIALS - 1:TRIALS]).then_inc(count_act, 1)

            with act.Fori(0, ROUNDS) as r:
                count_third(r, 1)
            act.wait_ge(dist_ready, 1)
            nc.scalar.activation(key_low, dist_bits[:, :, 0], ACT.Copy).then_inc(low_key_ready, 1)
            act.wait_ge(count_act, ROUNDS)
            nc.scalar.activation(signs, dist, ACT.Exp, scale=-1.0, accum_out=exp_sum[:, :]).then_inc(exp_sum_ready, 1)
            act.wait_ge(exp_sum_ready, 1)
            with act.Fori(ROUNDS, 2 * ROUNDS) as r:
                count_third(r, 2)
            act.wait_ge(denominator_ready, 1)
            nc.scalar.activation(log_sum[:, :], denominator[:, :], ACT.Ln).then_inc(log_sum_ready, 1)

            for c in range(FH // BANK):
                act.wait_ge(slotT_done, c + 1)
                nc.scalar.activation(flat_hi[:, c * BANK:(c + 1) * BANK], ps[:, c, :],
                                     ACT.Copy).then_inc(slot_copied, 1)

            def copy_fnT(m):
                act.wait_ge(fnT_done, m + 1)
                at_least(act, up_done, 3 * m)
                high_tokens(FNT, fnT_h_ready)

            def copy_wT(m):
                at_least(act, up_done, 3 * m)
                for s in range(3):
                    act.wait_ge(wT_done, 3 * m + s + 1)
                    nc.scalar.activation(wT[:, s, :, :, :].rearrange("p a k f -> p (a k f)"),
                                         ps[:, WT[s % 2], :].bitcast(F16)[:, 0:6 * P], ACT.Copy).then_inc(wT_ready, 1)

            def relu(m):
                at_least(act, down_done, m)
                for s in range(3):
                    act.wait_ge(up_done, 3 * m + s + 1)
                    nc.scalar.activation(hid_h[:, 2 * s:2 * s + 2, :].rearrange("p s t -> p (s t)"),
                                         ps[:, UP[s], 0:2 * N], ACT.Relu).then_inc(hid_h_ready, 1)

            def step2(n, q, i, on):
                if on(4):
                    relu(n - 4)
                if on(3):
                    copy_fnT(n - 3)
                    copy_wT(n - 3)

            over_images(act, UN, LAG2, step2)

        @block.vector
        def _(dve):
            nc.vector.memset(patches[0][32:64, :, 0:JH], 1.0).then_inc(pads_set, 1)
            nc.vector.memset(wtok_in[32:64, :, :], 0.0).then_inc(pads_set, 1)
            nc.vector.memset(patches[1][32:64, :, 0:JH], 1.0).then_inc(pads_set, 1)
            nc.vector.memset(eps[:, 0:1], EPS * S_TOK * S_TOK)
            nc.vector.memset(eps[:, 1:3], EPS)
            nc.vector.memset(mean_col[:, :], 1.0 / N)
            nc.vector.memset(yT_b[EB:EB + 1, :, :], 1.0)
            nc.vector.memset(sums[:, :, :], 1.0)
            nc.vector.memset(squares[:, :, :], 1.0)
            nc.vector.memset(limits[:, 0:TRIALS - 1], K - 0.5)
            nc.vector.memset(limits[:, TRIALS - 1:TRIALS], 2 * K - F - 0.5)
            nc.vector.memset(weights[:, 0:TRIALS - 1], 1.0)
            nc.vector.memset(weights[:, TRIALS - 1:TRIALS], 2.0).then_inc(fills_set, 1)

            def apart():
                dve.sem_inc(vector_passed)

            def collect(k, m, source, ready):
                dve.wait_ge(ready, m + 1)
                apart()
                for h in range(2):
                    last = nc.vector.bn_stats(stats[0:HALF, k, h, :], source(h))
                last.then_inc(ln_stats[k], 1)

            def aggregate(k, m):
                dve.wait_ge(ln_stats[k], m + 1)
                apart()
                for h in range(2):
                    last = nc.vector.bn_aggr(mv[0:HALF, k, h, :], stats[0:HALF, k, h, :])
                last.then_inc(ln_mv[k], 1)

            def invert(k, m):
                dve.wait_ge(ln_sd[k], m + 1)
                rstd = rs[0:HALF, k, :] if k < 2 else ffn_rstd[0:HALF, bass.ds(2 * m, 2)]
                nc.vector.reciprocal(rstd, sd[0:HALF, k, :]).then_inc(ln_rs[k], 1)

            def normalise(k, m, source, out_tile, out_ready, free):
                dve.wait_ge(ln_rs[k], m + 1)
                at_least(dve, free, m)
                for h in range(2):
                    r = rs[0:HALF, k, h:h + 1] if k < 2 else ffn_rstd[0:HALF, bass.ds(2 * m + h, 1)]
                    last = nc.vector.tensor_scalar(out_tile[0:HALF, h, :], source(h), mv[0:HALF, k, h, 0:1], r,
                                                   ALU.subtract, ALU.mult)
                last.then_inc(out_ready, 1)

            def embedded(p):
                return lambda h: ps[0:HALF, EMB[p], h * E:(h + 1) * E]

            def stream(m):
                return lambda h: image(m)[:, h, :]

            def attention_products(m):
                dve.wait_ge(sums_ready, m + 1)
                nc.vector.tensor_tensor(vq[:, 0, :], ps[:, V_AB, 0:N], q_s[:, 0, :], ALU.mult)
                nc.vector.tensor_tensor(vq[0:EB, 1, :], ps[0:EB, V_AB, N:2 * N], q_s[0:EB, 1, :],
                                        ALU.mult).then_inc(vq_ready, 1)
                nc.vector.tensor_tensor(sqsk[:, :], sums[:, 0, :], sums[:, 1, :], ALU.mult).then_inc(sqsk_ready, 1)

            def norm_products(m):
                dve.wait_ge(squares_ready, m + 1)
                nc.vector.tensor_tensor(roots_in[:, :], squares[:, 0, :], squares[:, 1, :],
                                        ALU.mult).then_inc(roots_in_ready, 1)

            def add_sums(m):
                dve.wait_ge(roots_ready, m + 1)
                dve.wait_ge(sqsk_ready, m + 1)
                nc.vector.scalar_tensor_tensor(out=denom[:, 0, :], in0=roots[:, 0, :], scalar=float(N),
                                               in1=sqsk[:, :], op0=ALU.mult,
                                               op1=ALU.add).then_inc(denom0_ready, 1)

            def multiply_by_k(m):
                dve.wait_ge(denom0_ready, m + 1)
                nc.vector.tensor_tensor(denom[:, 1, :], denom[:, 0, :], roots[:, 1, :],
                                        ALU.mult).then_inc(denom_ready, 1)

            def attention_result(m, p):
                dve.wait_ge(denom_ready, m + 1)
                nc.vector.reciprocal(coef[:, :], denom[:, 1, :]).then_inc(coef_ready, 1)
                dve.wait_ge(coef_ready, m + 1)
                dve.wait_ge(vq_ready, m + 1)
                at_least(dve, proj_done, m - 1)
                nc.vector.scalar_tensor_tensor(out=yT_a[:, p, :], in0=vq[:, 0, :], scalar=coef[:, 0:1],
                                               in1=k2[:, 0, :], op0=ALU.mult, op1=ALU.mult)
                nc.vector.scalar_tensor_tensor(out=yT_b[0:EB, p, :], in0=vq[0:EB, 1, :], scalar=coef[0:EB, 1:2],
                                               in1=k2[0:EB, 1, :], op0=ALU.mult,
                                               op1=ALU.mult).then_inc(y_ready, 1)

            def add_attention(m):
                dve.wait_ge(proj_done, m + 1)
                dve.wait_ge(hn_ready, m + 1)
                nc.vector.tensor_tensor(image(m), ps[0:HALF, PRJ, 0:2 * E].rearrange("p (h e) -> p h e", h=2),
                                        image(m), ALU.add).then_inc(resid_ready, 1)

            def keep_mean(m):
                nc.vector.tensor_copy(ffn_mean[0:HALF, bass.ds(2 * m, 2)], mv[0:HALF, 2, :, 0])

            def keep_pooled(m):
                dve.wait_ge(pool_done, m + 1)
                nc.vector.tensor_copy(pooled_a[:, bass.ds(m, 1)], ps[:, PRJ, POOLED:POOLED + 1])
                nc.vector.tensor_copy(pooled_b[:, bass.ds(m, 1)],
                                      ps[0:EB, PRJ, POOLED + 1:POOLED + 2]).then_inc(pool_kept, 1)

            dve.wait_ge(fills_set, 1)
            dve.wait_ge(wtok_h_ready, 1)
            nc.vector.scalar_tensor_tensor(out=wtok_l[0:KX, :, :], in0=wtok_in[0:KX, :, :], scalar=S_TOK,
                                           in1=wtok_h[0:KX, :, :], op0=ALU.mult,
                                           op1=ALU.subtract).then_inc(wtok_ready, 1)
            dve.wait_ge(wq_h_ready, 1)
            nc.vector.scalar_tensor_tensor(out=wq_al[:, :], in0=wq_in_a, scalar=S_QKV, in1=wq_ah[:, :],
                                           op0=ALU.mult, op1=ALU.subtract)
            nc.vector.scalar_tensor_tensor(out=wq_b[EB:P, :], in0=wq_in_b, scalar=S_QKV, in1=wq_b[0:EB, :],
                                           op0=ALU.mult, op1=ALU.subtract).then_inc(wq_ready, 1)

            def low_tokens(bank, ready):
                nc.vector.scalar_tensor_tensor(out=hnT_al[:, :], in0=ps[:, bank, 0:N], scalar=S_HN,
                                               in1=hnT_ah[:, :], op0=ALU.mult, op1=ALU.subtract)
                nc.vector.scalar_tensor_tensor(out=hnT_bl[:, :], in0=ps[0:EB, bank, 256:256 + N], scalar=S_HN,
                                               in1=hnT_bh[0:EB, :], op0=ALU.mult,
                                               op1=ALU.subtract).then_inc(ready, 1)

            def low_hnT(m):
                dve.wait_ge(hnT_h_ready, m + 1)
                at_least(dve, qkv_done, m)
                low_tokens(TRN, hnT_ready)

            def low_tab(c):
                dve.wait_ge(tab_h_ready, c + 1)
                for out_cols, src, high, scale in (
                    (slice(P, 2 * P), wm_in[:, 0:P], slice(0, P), S_MFC),
                    (slice(2 * P + EB, 2 * E), wm_in[:, P:E], slice(2 * P, 2 * P + EB), S_MFC),
                    (slice(3 * E, 4 * E), ps[0:CHUNK, TAB, 0:E], slice(2 * E, 3 * E), S_FFN),
                ):
                    last = nc.vector.scalar_tensor_tensor(out=tab_rows[:, out_cols], in0=src, scalar=scale,
                                                          in1=tab_rows[:, high], op0=ALU.mult, op1=ALU.subtract)
                last.then_inc(tab_ready, 1)

            def step1(n, p, i, on):
                if on(2):
                    collect(1, n - 2, stream(n - 2), h1_ready)
                if on(1):
                    collect(0, n - 1, embedded(1 - p), embed_done)
                if on(2):
                    aggregate(1, n - 2)
                if on(1):
                    aggregate(0, n - 1)
                if on(5):
                    add_attention(n - 5)
                if on(2):
                    invert(1, n - 2)
                if on(1):
                    invert(0, n - 1)
                if on(2):
                    normalise(1, n - 2, stream(n - 2), hn, hn_ready, hnT_done)
                if on(5):
                    collect(2, n - 5, stream(n - 5), resid_ready)
                if on(1):
                    normalise(0, n - 1, embedded(1 - p), z1, z1_ready, z2_ready)
                if on(5):
                    aggregate(2, n - 5)
                if p == 0 and on(2):
                    low_tab(i - 1)
                if on(6):
                    keep_pooled(n - 6)
                if on(3):
                    attention_products(n - 3)
                    norm_products(n - 3)
                if on(5):
                    invert(2, n - 5)
                    normalise(2, n - 5, stream(n - 5), hn2, hn2_ready, pool_done)
                    keep_mean(n - 5)
                if on(3):
                    add_sums(n - 3)
                    multiply_by_k(n - 3)
                    attention_result(n - 3, 1 - p)
                if on(2):
                    low_hnT(n - 2)

            over_images(dve, 2, LAG1, step1)

            done = 0

            def then(instruction):
                nonlocal done
                done += 1
                instruction.then_inc(sel_step, 1)
                dve.wait_ge(sel_step, done)

            scores = ps[:, 0:3, :].rearrange("p b c -> p (b c)")
            for c in range(FH // BANK):
                dve.wait_ge(scores_done, c + 1)
                last = nc.vector.tensor_reduce(tops[:, c:c + 1], ps[:, c, :], AX_X, ALU.max)
            then(last)
            nc.vector.tensor_reduce(top[:, :], tops[:, :], AX_X, ALU.max).then_inc(top_ready, 1)
            dve.wait_ge(cross_done, 1)
            dve.wait_ge(top_ready, 1)
            nc.vector.tensor_tensor(top_both[:, :], ps[:, CROSS, 0:1], top[:, :], ALU.max).then_inc(top_both_ready, 1)
            dve.wait_ge(top_both_ready, 1)
            nc.vector.tensor_scalar(dist, scores, top_both[:, :], -1.0, ALU.subtract, ALU.mult).then_inc(dist_ready, 1)
            dve.wait_ge(dist_ready, 1)
            then(nc.vector.tensor_copy(key, dist_bits[:, :, 1]))

            def search_round(r, turn, starts):
                dve.wait_ge(trial_ready, r + starts)
                for t in range(TRIALS - 1):
                    last = nc.vector.tensor_scalar(unread[t], key, trials[:, t:t + 1], 0.0, ALU.is_lt, ALU.add,
                                                   accum_out=counts[:, t:t + 1])
                last.then_inc(count_ready, 1)
                dve.wait_ge(bound_ready, r + starts)
                nc.vector.tensor_scalar(
                    next_trials[:, :], offsets[:, bass.ds(turn + 1, 1), :].rearrange("p r t -> p (r t)"),
                    bound[:, :], None, ALU.add).then_inc(next_ready, 1)
                dve.wait_ge(total_done, r + 1)
                nc.vector.scalar_tensor_tensor(out=kept[:, :], in0=ps[:, CROSS, 0:TRIALS], scalar=1.0,
                                               in1=limits[:, :], op0=ALU.mult, op1=ALU.is_lt,
                                               accum_out=steps_up[:, :]).then_inc(kept_ready, 1)
                dve.wait_ge(kept_ready, r + 1)
                dve.wait_ge(next_ready, r + 1)
                size = step_size[:, bass.ds(turn, 1)]
                nc.vector.scalar_tensor_tensor(out=trials[:, :], in0=size.to_broadcast([P, TRIALS]),
                                               scalar=steps_up[:, :], in1=next_trials[:, :], op0=ALU.mult,
                                               op1=ALU.add).then_inc(trial_ready, 1)
                nc.vector.scalar_tensor_tensor(out=bound[:, :], in0=size, scalar=steps_up[:, :], in1=bound[:, :],
                                               op0=ALU.mult, op1=ALU.add).then_inc(bound_ready, 1)

            def start_search():
                nc.vector.memset(bound[:, :], 0.0).then_inc(bound_ready, 1)
                nc.vector.tensor_copy(trials[:, :], offsets[:, 0, :]).then_inc(trial_ready, 1)

            dve.wait_ge(consts_set, 1)
            start_search()
            with dve.Fori(0, ROUNDS // 4) as four:
                for k in range(4):
                    search_round(4 * four + k, 4 * four + k, 1)
            dve.wait_ge(bound_ready, ROUNDS + 1)
            nc.vector.tensor_copy(bound_high[:, :], bound[:, :])
            nc.vector.tensor_scalar(unread[0], key, bound[:, :], 0.0, ALU.is_lt, ALU.add,
                                    accum_out=counts[:, 0:1]).then_inc(fewer_ready, 1)
            dve.wait_ge(fewer_ready, 1)
            then(nc.vector.tensor_scalar(unread[1], key, bound[:, :], float(2 ** 16 - 1), ALU.not_equal, ALU.mult))
            dve.wait_ge(low_key_ready, 1)
            then(nc.vector.tensor_tensor(key, unread[1], key_low, ALU.max))
            dve.wait_ge(cross_done, 3)
            nc.vector.tensor_copy(denominator[:, :], ps[:, CROSS, 1:2]).then_inc(denominator_ready, 1)
            then(nc.vector.tensor_scalar(fewer[:, :], ps[:, CROSS, 0:1], -1.0, None, ALU.mult))
            then(nc.vector.scalar_tensor_tensor(out=limits[:, :], in0=weights[:, :], scalar=fewer[:, :],
                                                in1=limits[:, :], op0=ALU.mult, op1=ALU.add))
            start_search()
            with dve.Fori(0, ROUNDS // 4) as four:
                for k in range(4):
                    search_round(ROUNDS + 4 * four + k, 4 * four + k, 2)
            dve.wait_ge(bound_ready, 2 * ROUNDS + 2)
            dve.wait_ge(count_act, 2 * ROUNDS)
            then(nc.vector.tensor_copy(bound_low[:, :], bound[:, :]))
            then(nc.vector.tensor_scalar(kth_bits[:, :], bound_high[:, :], 16, None, ALU.logical_shift_left))
            then(nc.vector.tensor_tensor(kth_bits[:, :], kth_bits[:, :], bound_low[:, :], ALU.bitwise_or))

            kth = kth_bits[:, :].bitcast(F32)
            dve.wait_ge(log_sum_ready, 1)
            then(nc.vector.tensor_scalar(underflow[:, :], log_sum[:, :], -1.0, EXP_UNDERFLOW, ALU.mult, ALU.add))
            then(nc.vector.tensor_tensor(kth, kth, underflow[:, :], ALU.min))
            nc.vector.tensor_scalar(below, dist, kth, 0.0, ALU.is_lt, ALU.add, accum_out=lt_count[:, :])
            nc.vector.scalar_tensor_tensor(out=tied, in0=dist, scalar=underflow[:, :],
                                           in1=kth.to_broadcast([P, FH]), op0=ALU.min, op1=ALU.is_equal,
                                           accum_out=eq_count[:, :]).then_inc(tie_counts_ready, 1)
            dve.wait_ge(tie_counts_ready, 1)
            dve.wait_ge(ones_set, 1)
            nc.vector.tensor_tensor_scan(running, ones, tied, 0.0, ALU.mult, ALU.add)
            dve.wait_ge(cross_done, 5)
            then(nc.vector.tensor_scalar(ties_left[:, :], ps[:, CROSS, 0:1], -1.0, float(K), ALU.mult, ALU.add))
            then(nc.vector.scalar_tensor_tensor(out=tied, in0=running, scalar=ties_left[:, :], in1=tied,
                                                op0=ALU.is_le, op1=ALU.mult))
            nc.vector.scalar_tensor_tensor(out=below, in0=below, scalar=1.0, in1=tied, op0=ALU.mult,
                                           op1=ALU.add, accum_out=chosen_count[:, :]).then_inc(chosen_ready, 1)
            dve.wait_ge(chosen_ready, 1)
            nc.vector.tensor_tensor_scan(running, ones, below, 0.0, ALU.mult, ALU.add)
            dve.wait_ge(cross_done, 6)
            then(nc.vector.tensor_scalar(chosen_before[:, :], ps[:, CROSS, 1:2], K_UP - 1.0, None, ALU.add))
            for c in range(FH // BANK):
                part = slice(c * BANK, (c + 1) * BANK)
                nc.vector.scalar_tensor_tensor(out=slots[:, part], in0=running[:, part], scalar=chosen_before[:, :],
                                               in1=below[:, part], op0=ALU.add,
                                               op1=ALU.mult).then_inc(slots_ready, 1)
            for c in range(FH // BANK):
                raw, low = (t[:, c * BANK:(c + 1) * BANK] for t in (flat_hi, flat_lo))
                dve.wait_ge(slot_copied, c + 1)
                then(nc.vector.tensor_scalar(low, raw, LO - 1, None, ALU.bitwise_and))
                last = nc.vector.tensor_scalar(raw, raw, LO.bit_length() - 1, None, ALU.arith_shift_right)
            last.then_inc(lohi_ready, 1)
            dve.wait_ge(lohi_ready, 1)

            def onehots(m):
                at_least(dve, list_done, m)
                at_least(dve, hi_vals_ready, m)
                lo_values, hi_values = iota32[:, 0:LO].unsqueeze(1), iota32[:, LO:LO + HI].unsqueeze(1)
                nc.vector.tensor_tensor(onehot_hi[:, :, :], hi_T[:, :, bass.ds(m, 1)].to_broadcast([P, NG, HI]),
                                        hi_values.to_broadcast([P, NG, HI]),
                                        ALU.is_equal).then_inc(onehot_ready, 1)
                nc.vector.tensor_tensor(onehot_lo[:, :, :], lo_T[:, :, bass.ds(m, 1)].to_broadcast([P, NG, LO]),
                                        lo_values.to_broadcast([P, NG, LO]), ALU.is_equal).then_inc(onehot_ready, 1)

            def list_values(m):
                dve.wait_ge(onehot_ready, 2 * m + 1)
                at_least(dve, list_done, m)
                nc.vector.tensor_tensor(hi_vals[:, :, 0, :], onehot_hi[:, :, :],
                                   group_no[:, :].unsqueeze(2).to_broadcast([P, NG, HI]), ALU.mult)
                nc.vector.tensor_scalar(hi_vals[:, :, 1, :], onehot_hi[:, :, :], feature_no[:, :], None,
                                   ALU.mult).then_inc(hi_vals_ready, 1)

            def write_index(m, q):
                dve.wait_ge(list_done, m + 1)
                at_least(dve, index_ready, m)
                nc.vector.tensor_scalar(groups_f[:, :], ps[0:LO, LIST, 0:HI], float(P), None,
                                        ALU.mult).then_inc(groups_f_ready, 1)
                dve.wait_ge(groups_f_ready, m + 1)
                g = (q - 2) % UN
                if isinstance(m, int):
                    at_least(dve, rows_in[g], 16 * SLOTS * ((m - 2) // UN + 1) if m >= 2 else 0)
                else:
                    dve.wait_ge(rows_in[g], (m - 2 - g) * (16 * SLOTS // UN) + 16 * SLOTS)
                for k in range(P // LO):
                    part = slice(k * SLOTS, (k + 1) * SLOTS)
                    last = nc.vector.tensor_tensor(index[q % 2][k * LO:(k + 1) * LO, :], groups_f[:, part],
                                                   ps[0:LO, LIST, HI + k * SLOTS:HI + (k + 1) * SLOTS], ALU.add)
                last.then_inc(index_ready, 1)

            def normalise_again(m):
                at_least(dve, fnT_done, m)
                for h in range(2):
                    last = nc.vector.tensor_scalar(hn2[0:HALF, h, :], image(m)[:, h, :],
                                                   ffn_mean[0:HALF, bass.ds(2 * m + h, 1)],
                                                   ffn_rstd[0:HALF, bass.ds(2 * m + h, 1)],
                                                   ALU.subtract, ALU.mult)
                last.then_inc(fn_ready, 1)

            def low_fnT(m):
                dve.wait_ge(fnT_h_ready, m + 1)
                at_least(dve, up_done, 3 * m)
                low_tokens(FNT, fnT_ready)

            def low_hidden(m):
                at_least(dve, down_done, m)
                for s in range(3):
                    dve.wait_ge(hid_h_ready, 3 * m + s + 1)
                    nc.vector.scalar_tensor_tensor(
                        out=hid_l[:, 2 * s:2 * s + 2, :].rearrange("p s t -> p (s t)"), in0=ps[:, UP[s], 0:2 * N],
                        scalar=0.0, in1=hid_h[:, 2 * s:2 * s + 2, :].rearrange("p s t -> p (s t)"),
                        op0=ALU.max, op1=ALU.subtract).then_inc(hid_ready, 1)

            def add_residual(m, q):
                dve.wait_ge(down_done, m + 1)
                if isinstance(m, int):
                    at_least(dve, stored[q % 2], 16 * (m // 2))
                else:
                    dve.wait_ge(stored[q % 2], (m - q % 2) * 8)
                nc.vector.scalar_tensor_tensor(
                    out=final[0:HALF, q % 2, :, :], in0=ps[0:HALF, DOWN, 0:2 * E].rearrange("p (h e) -> p h e", h=2),
                    scalar=1.0 / S_OUT, in1=image(m), op0=ALU.mult, op1=ALU.add).then_inc(final_ready, 1)

            def step2(n, q, i, on):
                if on(1):
                    write_index(n - 1, (q - 1) % UN)
                if on(4):
                    low_hidden(n - 4)
                if on(0):
                    onehots(n)
                    list_values(n)
                if on(3):
                    low_fnT(n - 3)
                if on(2):
                    normalise_again(n - 2)
                if on(4):
                    add_residual(n - 4, q)

            over_images(dve, UN, LAG2, step2)

        @block.tensor
        def _(pe):
            pe.wait_ge(consts_set, 1)
            pe.wait_ge(wtok_ready, 1)

            def transpose_w2():
                pe.wait_ge(fills_set, 1)
                pe.wait_ge(weights_in, 16 * N_WEIGHTS)
                for g in range(NG):
                    last = nc.tensor.transpose(ps[0:R, 2 + g // 4, (g % 4) * P:(g % 4 + 1) * P], w2_rows[:, g, :],
                                               ident[:, :])
                last.then_inc(w2T_done, 1)
                pe.wait_ge(w2T_ready, 1)
                pe.wait_ge(wq_ready, 1)

            def embed(n, p, h):
                if h == 0:
                    pe.wait_ge(x_h_ready, n + 1)
                    pe.wait_ge(x_l_ready, n + 1)
                    at_least(pe, z1_ready, n - 1)
                o = ps[0:HALF, EMB[p], h * E:(h + 1) * E]
                half = slice(h * HALF, (h + 1) * HALF)
                for j in range(JH):
                    nc.tensor.matmul(o, x_h[0:KX, p, half, j], wtok_h[0:KX, j, :], start=(j == 0), stop=False)
                    nc.tensor.matmul(o, x_h[0:KX, p, half, j], wtok_l[0:KX, j, :], start=False, stop=False)
                    last = nc.tensor.matmul(o, x_l[0:KX, p, half, j], wtok_h[0:KX, j, :], start=False,
                                            stop=(j == JH - 1))
                if h == 1:
                    last.then_inc(embed_done, 1)

            def transpose_tokens(bank, source):
                for h in range(2):
                    nc.tensor.transpose(ps[:, bank, h * HALF:(h + 1) * HALF], source[0:HALF, h, 0:P],
                                        ident[0:HALF, 0:HALF])
                    last = nc.tensor.transpose(ps[0:EB, bank, 256 + h * HALF:256 + (h + 1) * HALF],
                                               source[0:HALF, h, P:E], ident[0:HALF, 0:HALF])
                return last

            def channels_product(o, w_high, w_low, w_last):
                nc.tensor.matmul(o, w_high, hnT_ah[:, :], start=True, stop=False)
                nc.tensor.matmul(o, w_high, hnT_al[:, :], start=False, stop=False)
                nc.tensor.matmul(o, w_low, hnT_ah[:, :], start=False, stop=False)
                nc.tensor.matmul(o, w_last, hnT_bh[:, :], start=False, stop=False)
                return nc.tensor.matmul(o, w_last[0:EB], hnT_bl[:, :], start=False, stop=True)

            def transpose_normalised(m):
                pe.wait_ge(hn_ready, m + 1)
                at_least(pe, hnT_ready, m)
                transpose_tokens(TRN, hn).then_inc(hnT_done, 1)

            def qkv(m):
                pe.wait_ge(hnT_ready, m + 1)
                at_least(pe, vq_ready, m)
                at_least(pe, squares_ready, m)
                for out_ap, first, width in (
                    (ps[:, QK_A, 0:N], 0, P), (ps[:, QK_A, N:2 * N], P, P),
                    (ps[:, V_AB, 0:N], 2 * P, P), (ps[0:EB, V_AB, N:2 * N], 3 * P + 2 * EB, EB),
                    (ps[:, QK_B, 0:N], 3 * P, 2 * EB),
                ):
                    cols = slice(first, first + width)
                    last = channels_product(out_ap, wq_ah[:, cols], wq_al[:, cols], wq_b[:, cols])
                last.then_inc(qkv_done, 1)

            def project(m, p):
                pe.wait_ge(y_ready, m + 1)
                at_least(pe, resid_ready, m)
                at_least(pe, pool_kept, m - 1)
                for h in range(2):
                    o = ps[0:HALF, PRJ, h * E:(h + 1) * E]
                    half = slice(h * HALF, (h + 1) * HALF)
                    nc.tensor.matmul(o, yT_a[:, p, half], wp_a[:, :], start=True, stop=False)
                    last = nc.tensor.matmul(o, yT_b[:, p, half], wp_b[:, :], start=False, stop=True)
                last.then_inc(proj_done, 1)

            def pool_tokens(m):
                pe.wait_ge(hn2_ready, m + 1)
                pe.wait_ge(resid_ready, min(m + 2, B) if isinstance(m, int) else m + 2)
                for o, chans in ((ps[:, PRJ, POOLED:POOLED + 1], slice(0, P)),
                                 (ps[0:EB, PRJ, POOLED + 1:POOLED + 2], slice(P, E))):
                    for h in range(2):
                        last = nc.tensor.matmul(o, hn2[0:HALF, h, chans], mean_col[0:HALF, :],
                                                start=(h == 0), stop=(h == 1))
                last.then_inc(pool_done, 1)

            def transpose_tab(c):
                pe.wait_ge(tab_in, 48 * c + 48)
                at_least(pe, tab_ready, c)
                nc.tensor.transpose(ps[0:CHUNK, TAB, 0:P], wf_a[:, :], ident[:, :])
                nc.tensor.transpose(ps[0:CHUNK, TAB, P:E], wf_b[:, :],
                                    ident[0:EB, 0:EB]).then_inc(tabT_done, 1)

            def step1(n, p, i, on):
                if on(0):
                    embed(n, p, 0)
                if on(3):
                    qkv(n - 3)
                if p == 1 and on(0):
                    transpose_tab(i)
                if on(6):
                    pool_tokens(n - 6)
                if on(0):
                    embed(n, p, 1)
                if on(2):
                    transpose_normalised(n - 2)
                if on(4):
                    project(n - 4, p)

            over_images(pe, 2, LAG1, step1, after={0: transpose_w2})

            pe.wait_ge(pool_kept, B)
            pe.wait_ge(resid_ready, B)
            pe.wait_ge(y_ready, B)
            nc.tensor.matmul(ps[0:R, ROUTER, 0:B], w1T_a[:, :], pooled_a[:, :], start=True, stop=False)
            nc.tensor.matmul(ps[0:R, ROUTER, 0:B], w1T_b[:, :], pooled_b[:, :], start=False,
                             stop=True).then_inc(router_done, 1)
            pe.wait_ge(router_ready, 1)
            for c in range(FH // BANK):
                for h in range(2):
                    last = nc.tensor.matmul(ps[h * B:(h + 1) * B, c, :], router[:, :],
                                            w2T[h][:, c * BANK:(c + 1) * BANK], start=True, stop=True)
                last.then_inc(scores_done, 1)
            pe.wait_ge(top_ready, 1)
            nc.tensor.matmul(ps[:, CROSS, 0:1], swap[:, :], top[:, :], start=True, stop=True).then_inc(cross_done, 1)
            pe.wait_ge(top_both_ready, 1)

            def total(r):
                pe.wait_ge(count_ready, r + 1)
                pe.wait_ge(count_act, r + 1)
                at_least(pe, kept_ready, r)
                nc.tensor.matmul(ps[:, CROSS, 0:TRIALS], pair[:, :], counts[:, :], start=True,
                                 stop=True).then_inc(total_done, 1)

            total(0)
            with pe.Fori(1, ROUNDS) as r:
                total(r)
            pe.wait_ge(fewer_ready, 1)
            nc.tensor.matmul(ps[:, CROSS, 0:1], pair[:, :], counts[:, 0:1], start=True,
                             stop=True).then_inc(cross_done, 1)
            pe.wait_ge(exp_sum_ready, 1)
            nc.tensor.matmul(ps[:, CROSS, 1:2], pair[:, :], exp_sum[:, :], start=True,
                             stop=True).then_inc(cross_done, 1)
            with pe.Fori(ROUNDS, 2 * ROUNDS) as r:
                total(r)

            pe.wait_ge(tie_counts_ready, 1)
            nc.tensor.matmul(ps[:, CROSS, 0:1], pair[:, :], lt_count[:, :], start=True,
                             stop=False).then_inc(cross_done, 1)
            nc.tensor.matmul(ps[:, CROSS, 0:1], lower[:, :], eq_count[:, :], start=False,
                             stop=True).then_inc(cross_done, 1)
            pe.wait_ge(chosen_ready, 1)
            nc.tensor.matmul(ps[:, CROSS, 1:2], lower[:, :], chosen_count[:, :], start=True,
                             stop=True).then_inc(cross_done, 1)
            for c in range(NCH):
                if c % 4 == 0:
                    pe.wait_ge(slots_ready, c // 4 + 1)
                last = nc.tensor.transpose(ps[:, c // 4, (c % 4) * P:(c % 4 + 1) * P], slots[:, c * P:(c + 1) * P],
                                           ident[:, :])
                if c % 4 == 3:
                    last.then_inc(slotT_done, 1)

            pe.wait_ge(lohi_ready, 1)

            def up(m):
                pe.wait_ge(fnT_ready, m + 1)
                pe.wait_ge(wT_ready, 3 * m + 3)
                at_least(pe, hid_ready, 3 * m)
                for s in range(3):
                    for k in range(2):
                        last = channels_product(ps[:, UP[s], k * N:(k + 1) * N], wT[:, s, 0, k, :],
                                                wT[:, s, 1, k, :], wT[:, s, 2, k, :])
                    last.then_inc(up_done, 1)

            def transpose_renormalised(m):
                pe.wait_ge(fn_ready, m + 1)
                at_least(pe, fnT_ready, m)
                transpose_tokens(FNT, hn2).then_inc(fnT_done, 1)

            def transpose_rows(m, g, groups):
                if isinstance(m, int):
                    pe.wait_ge(rows_in[g], 16 * SLOTS * (m // UN + 1))
                else:
                    pe.wait_ge(rows_in[g], (m - g) * (16 * SLOTS // UN) + 16 * SLOTS)
                for s in groups:
                    at_least(pe, wT_ready, 3 * m + s - 1)
                    for k in range(2):
                        for a in range(3):
                            first = (2 * a + k) * P
                            last = nc.tensor.transpose(ps[:, WT[s % 2], :].bitcast(F16)[:, first:first + P],
                                                       gathered[g][:, 2 * s + k, a * P:(a + 1) * P], ident16[:, :])
                    last.then_inc(wT_done, 1)

            def make_list(m):
                pe.wait_ge(hi_vals_ready, m + 1)
                pe.wait_ge(onehot_ready, 2 * m + 2)
                at_least(pe, index_ready, m)
                for g in range(NG):
                    last = nc.tensor.matmul(ps[0:LO, LIST, 0:2 * HI], onehot_lo[:, g, :],
                                            hi_vals[:, g, :, :].rearrange("p a h -> p (a h)"),
                                            start=(g == 0), stop=(g == NG - 1))
                last.then_inc(list_done, 1)

            def down(m, g, h):
                if h == 0:
                    at_least(pe, final_ready, m)
                o = ps[0:HALF, DOWN, h * E:(h + 1) * E]
                half = slice(h * HALF, (h + 1) * HALF)
                for s in range(SLOTS):
                    if h == 0 and s % 2 == 0:
                        pe.wait_ge(hid_ready, 3 * m + s // 2 + 1)
                    w_high, w_low = gathered[g][:, s, 2 * E:3 * E], gathered[g][:, s, 3 * E:4 * E]
                    nc.tensor.matmul(o, hid_h[:, s, half], w_high, start=(s == 0), stop=False)
                    nc.tensor.matmul(o, hid_h[:, s, half], w_low, start=False, stop=False)
                    last = nc.tensor.matmul(o, hid_l[:, s, half], w_high, start=False, stop=(s == SLOTS - 1))
                if h == 1:
                    last.then_inc(down_done, 1)

            def step2(n, q, i, on):
                if on(1):
                    make_list(n - 1)
                if on(4):
                    up(n - 4)
                if on(3):
                    transpose_renormalised(n - 3)
                    transpose_rows(n - 3, (q - 3) % UN, (0, 1))
                if on(4):
                    down(n - 4, q, 0)
                if on(3):
                    transpose_rows(n - 3, (q - 3) % UN, (2,))
                if on(4):
                    down(n - 4, q, 1)

            over_images(pe, UN, LAG2, step2)


_INS = ['x', 'L0_tok_w_proj', 'L0_tok_b_proj', 'L0_tok_ln_gamma', 'L0_tok_ln_beta', 'L0_attn_w_qkv',
        'L0_attn_w_proj', 'L0_attn_b_proj', 'L0_ffn_w1', 'L0_ffn_w2', 'L0_ffn_w_mfc', 'L0_ffn_w_proj']
_OUT = ((64, 196, 192), 'float32')


def kernel(**inputs):
    import numpy as _np
    import concourse.bacc as _bacc
    from concourse import mybir as _mybir
    from concourse.bass_utils import run_bass_kernel_spmd as _run

    nc = _bacc.Bacc("TRN2", target_bir_lowering=False, num_devices=1)
    arrays, args = {}, []
    for name in _INS:
        a = _np.ascontiguousarray(inputs[name])
        arrays[f"in_{name}_dram"] = a
        args.append(nc.dram_tensor(f"in_{name}_dram", a.shape, _mybir.dt.from_np(a.dtype), kind="ExternalInput").ap())
    shape, dtype = _OUT
    args.append(nc.dram_tensor("out_dram", shape, _mybir.dt.from_np(_np.dtype(dtype)), kind="ExternalOutput").ap())
    vit_tower(nc, *args)
    r = _run(nc, [arrays], core_ids=[0])
    return r.results[0]["out_dram"]
```
